# Optimizing a Trainium2 kernel written in Bass

```python
import numpy as np
import jax
import jax.numpy as jnp

def _softmax(x, axis=-1):
    return jax.nn.softmax(x, axis=axis)

def _gelu(x):
    return jax.nn.gelu(x, approximate=True)

def _silu(x):
    return jax.nn.silu(x)

def _sigmoid(x):
    return jax.nn.sigmoid(x)

def _layernorm(x, axis=-1, eps=1e-05):
    m = jnp.mean(x, axis=axis, keepdims=True)
    v = jnp.var(x, axis=axis, keepdims=True)
    return (x - m) / jnp.sqrt(v + eps)

def _scatter_add(tgt, idx, src, axis=0):
    return tgt.at[idx].add(src)

def _segment_sum(src, seg, n):
    return jax.ops.segment_sum(src, seg, n)
kernel_name = 'mk_decoder_postln_d1_seqx_r8_bd2539'

def setup_inputs(seed: int=0):
    np.random.seed(seed)
    _w = jnp.asarray

    def _rec_inputs():
        import jax
        import jax.numpy as jnp
        _rk = jax.random.key(seed)
        x = 4.136e-05 + 0.9999 * jax.random.normal(jax.random.fold_in(_rk, 1), (8, 128, 128), jnp.float32)
        _lenS = 128 - jax.random.randint(jax.random.fold_in(_rk, 7), (8,), 0, max(1, 128 // 4) + 1, jnp.int32)
        _lenS2 = 128 - jax.random.randint(jax.random.fold_in(_rk, 8), (8,), 0, max(1, 128 // 4) + 1, jnp.int32)
        _ctx_2048P = jax.random.normal(jax.random.fold_in(_rk, 11), (8, 16, 256), jnp.float32)
        _ctx_2048c = jax.random.dirichlet(jax.random.fold_in(_rk, 511), 0.3 * jnp.ones((16,), jnp.float32), (8, 128))
        _ctx_2048t = jnp.einsum('bsk,bkd->bsd', _ctx_2048c, _ctx_2048P)
        _ctx_2048t = _ctx_2048t * jax.lax.rsqrt(jnp.mean(jnp.square(_ctx_2048t)) + 1e-12) * 0.953939
        ctx_2048 = -0.000392918 + 0.999932 * (_ctx_2048t + 0.3 * jax.random.normal(jax.random.fold_in(_rk, 611), (8, 128, 256), jnp.float32))
        itok_Bx1_68_817 = jax.random.randint(jax.random.fold_in(_rk, 12), (8, 1), 68, 818, jnp.int32)
        return (x, ctx_2048, itok_Bx1_68_817)
    x, ctx_2048, itok_Bx1_68_817 = _rec_inputs()

    def _L0_attn_setup():
        import jax, jax.numpy as jnp
        import numpy as np
        DIM = 128
        HEADS = 16
        DIM_HEAD = 64
        B, S = (4, 256)
        key = jax.random.key(seed)
        ks = jax.random.split(key, 6)
        sd = 1.0 / np.sqrt(DIM)
        return {'latents': jax.random.normal(ks[0], (B, S, DIM), dtype=jnp.float32), 'ln_gamma': jnp.ones((DIM,), dtype=jnp.float32), 'ln_beta': jnp.zeros((DIM,), dtype=jnp.float32), 'Wq': jax.random.normal(ks[1], (DIM, HEADS * DIM_HEAD), dtype=jnp.float32) * sd, 'Wk': jax.random.normal(ks[2], (DIM, HEADS * DIM_HEAD), dtype=jnp.float32) * sd, 'Wv': jax.random.normal(ks[3], (DIM, HEADS * DIM_HEAD), dtype=jnp.float32) * sd, 'Wo': jax.random.normal(ks[4], (HEADS * DIM_HEAD, DIM), dtype=jnp.float32) * sd}
    _L0_attn_all = _L0_attn_setup()
    _L0_attn_in = {k: v for k, v in _L0_attn_all.items() if k in ('ln_gamma', 'ln_beta', 'Wq', 'Wk', 'Wv', 'Wo')}
    del _L0_attn_all

    def _L0_xattn_setup():
        import jax, jax.numpy as jnp
        import numpy as np
        UNITS = 128
        NUM_HEADS = 16
        MASK_VALUE = -1000000000000.0

        def _split_heads(x, n):
            B, S, D = x.shape
            return x.reshape(B, S, n, D // n).transpose(0, 2, 1, 3)
        key = jax.random.key(seed)
        k1, k2, k3, k4 = jax.random.split(key, 4)
        B, S = (8, 128)
        memory = jax.random.normal(k1, (B, S, 2 * UNITS), dtype=jnp.float32)
        query = jax.random.normal(k2, (B, S, UNITS), dtype=jnp.float32)
        b = jax.random.normal(k3, (S,), dtype=jnp.float32)
        seq_len = jax.random.randint(k4, (B, 1), 0, S, dtype=jnp.int32)
        return {'memory': memory, 'query': query, 'b': b, 'seq_len': seq_len}
    _L0_xattn_all = _L0_xattn_setup()
    _L0_xattn_in = {k: v for k, v in _L0_xattn_all.items() if k in ('b',)}
    del _L0_xattn_all

    def _L0_ffn_setup():
        import jax, jax.numpy as jnp
        import numpy as np
        TOP_K = 2
        key = jax.random.key(seed)
        ks = jax.random.split(key, 5)
        B, S, H, I, E = (4, 512, 128, 256, 8)
        scale = 0.02
        return {'hidden_states': jax.random.normal(ks[0], (B, S, H), dtype=jnp.float32), 'router_w': jax.random.normal(ks[1], (E, H), dtype=jnp.float32) * scale, 'gate_w': jax.random.normal(ks[2], (E, I, H), dtype=jnp.float32) * scale, 'up_w': jax.random.normal(ks[3], (E, I, H), dtype=jnp.float32) * scale, 'down_w': jax.random.normal(ks[4], (E, H, I), dtype=jnp.float32) * scale}
    _L0_ffn_all = _L0_ffn_setup()
    _L0_ffn_in = {k: v for k, v in _L0_ffn_all.items() if k in ('router_w', 'gate_w', 'up_w', 'down_w')}
    del _L0_ffn_all
    return {'x': x, 'ctx_2048': ctx_2048, 'itok_Bx1_68_817': itok_Bx1_68_817, 'L0_attn_ln_gamma': _L0_attn_in['ln_gamma'], 'L0_attn_ln_beta': _L0_attn_in['ln_beta'], 'L0_attn_Wq': _L0_attn_in['Wq'], 'L0_attn_Wk': _L0_attn_in['Wk'], 'L0_attn_Wv': _L0_attn_in['Wv'], 'L0_attn_Wo': _L0_attn_in['Wo'], 'L0_xattn_b': _L0_xattn_in['b'], 'L0_ffn_router_w': _L0_ffn_in['router_w'], 'L0_ffn_gate_w': _L0_ffn_in['gate_w'], 'L0_ffn_up_w': _L0_ffn_in['up_w'], 'L0_ffn_down_w': _L0_ffn_in['down_w']}

def reference(x, ctx_2048, itok_Bx1_68_817, L0_attn_ln_gamma, L0_attn_ln_beta, L0_attn_Wq, L0_attn_Wk, L0_attn_Wv, L0_attn_Wo, L0_xattn_b, L0_ffn_router_w, L0_ffn_gate_w, L0_ffn_up_w, L0_ffn_down_w):
    import jax
    import jax.numpy as jnp

    def _L0_attn_ref(latents, ln_gamma, ln_beta, Wq, Wk, Wv, Wo):
        import jax, jax.numpy as jnp
        import numpy as np
        DIM = 128
        HEADS = 16
        DIM_HEAD = 64
        B, S = (4, 256)
        mu = jnp.mean(latents, axis=-1, keepdims=True)
        var = jnp.mean((latents - mu) ** 2, axis=-1, keepdims=True)
        x = (latents - mu) * jax.lax.rsqrt(var + 1e-05) * ln_gamma + ln_beta
        b, s, _ = x.shape
        q = (x @ Wq).reshape(b, s, HEADS, DIM_HEAD).transpose(0, 2, 1, 3)
        k = (x @ Wk).reshape(b, s, HEADS, DIM_HEAD).transpose(0, 2, 1, 3)
        v = (x @ Wv).reshape(b, s, HEADS, DIM_HEAD).transpose(0, 2, 1, 3)
        scale = 1.0 / np.sqrt(np.sqrt(DIM_HEAD))
        scores = jnp.einsum('bhqd,bhkd->bhqk', q * scale, k * scale)
        weights = jax.nn.softmax(scores.astype(jnp.float32), axis=-1).astype(scores.dtype)
        out = jnp.einsum('bhqk,bhkd->bhqd', weights, v)
        out = out.transpose(0, 2, 1, 3).reshape(b, s, HEADS * DIM_HEAD)
        return out @ Wo

    def _L0_xattn_ref(memory, query, b, seq_len):
        import jax, jax.numpy as jnp
        import numpy as np
        UNITS = 128
        NUM_HEADS = 16
        MASK_VALUE = -1000000000000.0

        def _split_heads(x, n):
            B, S, D = x.shape
            return x.reshape(B, S, n, D // n).transpose(0, 2, 1, 3)
        B, S, _ = query.shape
        dh = UNITS // NUM_HEADS
        k_mem, v_mem = jnp.split(memory, 2, axis=2)
        Q = _split_heads(query, NUM_HEADS) * dh ** (-0.5)
        Kh = _split_heads(k_mem, NUM_HEADS)
        Vh = _split_heads(v_mem, NUM_HEADS)
        logits = jnp.einsum('bhqd,bhkd->bhqk', Q, Kh) + b
        valid = (jnp.arange(S)[None, :] < seq_len[:, 0:1]).astype(jnp.float32)
        logits = logits + MASK_VALUE * (1.0 - valid)[:, None, None, :]
        weights = jax.nn.softmax(logits, axis=-1)
        out = jnp.einsum('bhqk,bhkd->bhqd', weights, Vh)
        return out.transpose(0, 2, 1, 3).reshape(B, S, UNITS)

    def _L0_ffn_ref(hidden_states, router_w, gate_w, up_w, down_w):
        import jax, jax.numpy as jnp
        import numpy as np
        TOP_K = 2
        B, S, H = hidden_states.shape
        E = router_w.shape[0]
        flat = hidden_states.reshape(-1, H)
        logits = flat @ router_w.T
        probs = jax.nn.softmax(logits.astype(jnp.float32), axis=-1)
        topk_prob, topk_idx = jax.lax.top_k(probs, TOP_K)
        topk_prob = topk_prob / jnp.sum(topk_prob, axis=-1, keepdims=True)
        topk_prob = topk_prob.astype(logits.dtype)
        out = jnp.zeros_like(flat)
        for e in range(E):
            w_e = jnp.sum(topk_prob * (topk_idx == e), axis=-1)
            g = jax.nn.silu(flat @ gate_w[e].T)
            u = flat @ up_w[e].T
            y = g * u @ down_w[e].T
            out = out + w_e[:, None] * y
        return out.reshape(B, S, H)
    x = _layernorm(x + _L0_attn_ref(x, L0_attn_ln_gamma, L0_attn_ln_beta, L0_attn_Wq, L0_attn_Wk, L0_attn_Wv, L0_attn_Wo), axis=-1)
    x = _layernorm(x + _L0_xattn_ref(ctx_2048, x, L0_xattn_b, itok_Bx1_68_817), axis=-1)
    x = _layernorm(x + _L0_ffn_ref(x, L0_ffn_router_w, L0_ffn_gate_w, L0_ffn_up_w, L0_ffn_down_w), axis=-1)
    return x

_drawn_inputs = setup_inputs


def setup_inputs(seed=0):
    import zlib

    import numpy as np

    out = dict(_drawn_inputs(seed))
    spreads = {'L0_attn_ln_gamma': (1.0, 0.2), 'L0_attn_ln_beta': (0.0, 0.1)}
    factors = {'L0_ffn_router_w': 8.0, 'L0_ffn_gate_w': 8.0, 'L0_ffn_up_w': 8.0, 'L0_ffn_down_w': 8.0}
    for name, (base, spread) in spreads.items():
        noise = np.random.default_rng([zlib.crc32(name.encode()), seed]).standard_normal(out[name].shape)
        drawn = base * np.exp(spread * noise) if base else spread * noise
        out[name] = jnp.asarray(drawn.astype(out[name].dtype))
    for name, factor in factors.items():
        out[name] = (out[name] * factor).astype(out[name].dtype)
    return out
```

```python
from contextlib import ExitStack

import concourse.bass as bass
from concourse import mybir

F32 = mybir.dt.float32
F32R = mybir.dt.float32r
BF16 = mybir.dt.bfloat16
I32 = mybir.dt.int32
U32 = mybir.dt.uint32
ALU = mybir.AluOpType
ACT = mybir.ActivationFunctionType
AX_X = mybir.AxisListType.X

P = 128
B = 8
D = 128
H = 16
DH = 64
HU = 4
UB = H // HU
NS = B * UB
NU = 2 * NS
GB = 2
NT = (B // GB) * (H // 2)
TLEAD = H // 2
XH = D // H
PARTS = 3
KROWS = PARTS * PARTS * XH
KALL = KROWS + 2 * PARTS
EPS = 1e-5
E = 8
FI = 256
NTOK = B * P
NBLK = (2 * NTOK + E * (P - 1)) // P

PT_LAG, PV_LAG = 2, 3


def mask_parts():
    import numpy as np
    rest, out = np.float32(-1e12), []
    for _ in range(PARTS):
        top = np.array([rest], np.float32).view(np.uint32) & np.uint32(0xFFFF0000)
        out.append(float(top.view(np.float32)[0]))
        rest = np.float32(rest - np.float32(out[-1]))
    assert rest == 0
    return out


def decoder_layer(nc, x, ctx_in, seq_len, gamma, beta, wq, wk, wv, wo, key_bias, router_w, gate_w, up_w,
                  down_w, out):
    stack = ExitStack()
    with stack:
        sem = lambda name: stack.enter_context(nc.semaphore(name))
        KB = 1024
        base = (nc.sbuf_base + 63) // 64 * 64
        ARENA = 207 * KB
        stack.enter_context(nc.sbuf_tensor("arena", [P, ARENA // 4 + 16], F32))

        def at(name, kb, shape, dt):
            size = {F32: 4, F32R: 4, BF16: 2, I32: 4, U32: 4}[dt]
            n = size
            for s in shape[1:]:
                n *= s
            assert kb * KB + n <= ARENA, name
            return nc.alloc_sbuf_tensor_at(name, shape, dt, offset=base + int(kb * KB))

        X = at("X", 0, [P, B, D], F32)
        X2 = at("X2", 0, [P, B, D], F32)
        X1 = at("X1", 4, [P, B, D], F32)
        XTh = at("XTh", 8, [D, NTOK], F32R)
        XTl = at("XTl", 12, [D, NTOK], F32R)
        CV = at("CV", 16, [P, B, D], F32)
        QP = at("QP", 20, [P, H, NTOK], BF16)
        KP = at("KP", 52, [P, H, NTOK], BF16)
        Mh = at("Mh", 84, [D, H, D], F32R)
        Ml = at("Ml", 92, [D, H, D], F32R)
        Vh = at("Vh", 100, [D, H, D], F32R)
        Vl = at("Vl", 108, [D, H, D], F32R)
        Th = at("Th", 116, [D, 2, GB, H, P], F32R)
        Tl = at("Tl", 148, [D, 2, GB, H, P], F32R)
        VP = at("VP", 180, [P, 3, HU * D], F32)
        EX = at("EX", 186, [P, 3, HU * P], F32)
        PTs = at("PTs", 192, [P, 3, HU * P], F32)
        WK = at("WK", 132, [P, H * DH], F32)
        WQ = at("WQ", 136, [P, H * DH], F32)
        WV = at("WV", 140, [P, H * DH], F32)
        WKT = at("WKT", 144, [P, 8, D], F32)
        WVT = at("WVT", 164, [P, 8, D], F32)
        WQBD = at("WQBD", 168, [P, 8, 2, D], F32)
        WOBD = at("WOBD", 186, [P, 8, 2, D], F32)
        XHAT = at("XHAT", 20, [P, B, D], F32)
        XTF = at("XTF", 24, [D, NTOK], F32)
        CK = at("CK", 28, [P, B, D], F32)
        CKR = at("CKR", 32, [P, B, D], F32)
        CKP = at("CKP", 36, [P, PARTS, B, D], BF16)
        KTP = at("KTP", 42, [D, PARTS, NTOK], BF16)
        VPAD = at("VPAD", 116, [P, 2, H, D], F32)
        WGUh = at("WGUh", 148, [D, E, 2, FI], F32R)
        WGUl = at("WGUl", 132, [D, E, 2, FI], F32R)
        WD = at("WD", 164, [P, E, 2, D], F32)
        GRAW = at("GRAW", 84, [P, 2 * E, D], F32)
        URAW = at("URAW", 92, [P, 2 * E, D], F32)
        DRAW = at("DRAW", 100, [P, E, 2, P], F32)
        XG = at("XG", 52, [P, 4, D], F32)
        XGTh = at("XGTh", 54, [D, 2, P], F32R)
        XGTl = at("XGTl", 55, [D, 2, P], F32R)
        SG = at("SG", 56, [P, 2, FI], F32)
        HUs = at("HUs", 58, [P, 2, FI], F32)
        HT = at("HT", 60, [P, 2, 2, P], F32)
        YS = at("YS", 62, [P, 4, D], F32)
        G1 = at("G1", 20, [P, B, D], F32)
        G2 = at("G2", 24, [P, B, D], F32)
        Z = at("Z", 28, [P, B, D], F32)
        OUT = at("OUT", 32, [P, B, D], F32)
        ID = at("ID", 198, [P, P], F32)
        IDB = at("IDB", 198.5, [P, P], BF16)
        Y = at("Y", 198.75, [P, 2, D], F32)
        QB = at("QB", 199.75, [P, PARTS, D], BF16)
        QT = at("QT", 200.5, [P, 2, PARTS, P], BF16)
        QR = at("QR", 202, [P, D], F32)
        X2T = at("X2T", 202.5, [D, P], F32)
        UT = at("UT", 203, [P, P], BF16)
        ONES = at("ONES", 203.25, [P, P], BF16)
        ZERO = at("ZERO", 203.5, [P, D], F32)
        cur = [204 * KB]

        def small(name, shape, dt=F32):
            n = 2 if dt == BF16 else 4
            for s in shape[1:]:
                n *= s
            t = nc.alloc_sbuf_tensor_at(name, shape, dt, offset=base + int(cur[0]))
            cur[0] += (n + 31) // 32 * 32
            assert cur[0] <= ARENA, name
            return t

        GB_ = small("GB_", [P, 2])
        HALF = small("HALF", [P, B])
        NMX = small("NMX", [P, 4, HU])
        SUM = small("SUM", [P, 4, HU])
        RCP = small("RCP", [P, 4, HU])
        BST = small("BST", [P, B, 6])
        BMV = small("BMV", [P, B, 2])
        VE = small("VE", [P, B])
        RS = small("RS", [P, B])
        TST = small("TST", [P, 6])
        TMV = small("TMV", [P, 2, 2])
        TVE = small("TVE", [P, 2])
        TRS = small("TRS", [P, 2])
        RW = small("RW", [D, E])
        rt = [36 * KB]

        def table(name, shape, dt=F32):
            n = 2 if dt == BF16 else 4
            for s in shape[1:]:
                n *= s
            t = nc.alloc_sbuf_tensor_at(name, shape, dt, offset=base + rt[0])
            rt[0] += (n + 31) // 32 * 32
            assert rt[0] <= 52 * KB
            return t

        LG, PE_, EQ, OH1, OH2, SL = (table(n, [P, B, E]) for n in ("LG", "PE_", "EQ", "OH1", "OH2", "SL"))
        ROWS = table("ROWS", [P, 12, B])
        AB = table("AB", [P, B, E], BF16)
        WTE = table("WTE", [P, B, E])
        THR = table("THR", [P, E, 8])
        TRI = table("TRI", [P, E, E])
        CMP = table("CMP", [P, NBLK + 1, E])
        BLK = table("BLK", [P, NBLK + 1, E])
        CNT = table("CNT", [P, 4, E])
        EIDF = table("EIDF", [P, NBLK + 1])
        EID = table("EID", [P, NBLK + 1], I32)
        SLOT = table("SLOT", [P, 2, B], U32)
        BROW = at("BROW", 48, [1, P], F32)
        BRES = at("BRES", 48.5, [1, P], F32)
        BPT = at("BPT", 49, [1, PARTS, P], BF16)
        SLI = at("SLI", 50, [B, 1], I32)
        SLF = at("SLF", 50.25, [B, 1], F32)
        KIX = at("KIX", 50.5, [B, P], F32)
        MPT = at("MPT", 51, [B, PARTS, P], BF16)

        bank = [stack.enter_context(nc.psum_tensor(f"bank{i}", [P, 512], F32)) for i in range(8)]
        T_BANK, V_BANK, S_BANK, PT_BANK, ACC, MISC = 0, 1, (2, 3), (4, 5), 6, 7

        dram = lambda name, shape, dt: nc.dram_tensor(name, shape, dt, kind="Internal").ap()
        k_scr = dram("k_scr", [PARTS, D, NTOK], BF16)
        q_scr = dram("q_scr", [B, D, PARTS, P], BF16)
        b_scr = dram("b_scr", [PARTS, P], BF16)
        m_scr = dram("m_scr", [B, PARTS, P], BF16)
        x_slots = dram("x_slots", [NBLK * P, D], F32)
        y_slots = dram("y_slots", [NBLK * P, D], F32)

        names = """x_in wk_in wq_in wv_in wo_in gb_in ck_in cv_in rw_in rows_in gate_in up_in down_in
            ident zeroed consts stats_x rstd_x xhat_done chain setup_full xtf_done xth_done xtl_done
            mh_done oh_done t_full th_done tl_done s_full max_done exp_done sum_recip p_norm v_full v_done
            pt_full pt_done pv_full y_added var_ready rstd_ready x_normed misc_full misc_done parts_ready
            ck_parts rows_ready k_scr_in rows_scr_in kp_in q_ones vpad_zero vpad_done w_full wh_done w_done
            router_full route_exp a_ready rank_full slots_ready x_scattered eid_ready slots_zero
            xgt_full xgh_done xgl_done gu_full silu_done hu_done ht_full ht_done dn_full y_done
            gathered z_done last_var last_rstd out_ready stored split_q route_l zero_tile""".split()
        s = {n: sem(n) for n in names}
        set_done = [sem(f"setup_done{i}") for i in range(16)]
        q_scr_in = [sem(f"q_scr_in{b}") for b in range(B)]
        q_in = [sem(f"q_in{b}") for b in range(B)]
        xg_in = [sem(f"xg_in{i}") for i in range(4)]
        y_out = [sem(f"y_out{i}") for i in range(4)]
        block = stack.enter_context(nc.Block())

        K0, Q0, X0, M0, WV0, O0 = 0, 2, 4, 6, 10, 12
        N_SETUP = 16
        sbank = lambda i: bank[2 + i % 4]
        unit = lambda n: (n // UB % B, n % UB)
        TAIL = 6

        @block.sync
        def _(sp):
            sp.dma_start(X[:, :, :], x.rearrange("b s d -> s b d")).then_inc(s["x_in"], 16)
            sp.dma_start(WQ[:, :], wq).then_inc(s["wq_in"], 16)
            sp.dma_start(WV[:, :], wv).then_inc(s["wv_in"], 16)
            sp.wait_ge(s["zeroed"], 2)
            for j in range(2):
                sp.dma_start(WOBD[DH * j:DH * j + DH, :, j, :],
                             wo.rearrange("(c j p) n -> j p c n", j=2, p=DH)[j]).then_inc(s["wo_in"], 16)
            sp.dma_start(CK[:, :, :], ctx_in[:, :, 0:D].rearrange("b s d -> s b d")).then_inc(s["ck_in"], 16)
            sp.dma_start(BROW[:, :], key_bias.rearrange("(a k) -> a k", a=1)).then_inc(s["rows_in"], 16)
            sp.dma_start(SLI[:, :], seq_len).then_inc(s["rows_in"], 16)
            sp.dma_start(CV[:, :, :], ctx_in[:, :, D:2 * D].rearrange("b s d -> s b d")).then_inc(s["cv_in"], 16)
            sp.wait_ge(s["rows_ready"], 1)
            sp.dma_start(b_scr.rearrange("(a p) k -> a p k", a=1), BPT[:, :, :]).then_inc(s["rows_scr_in"], 16)
            sp.dma_start(m_scr, MPT[:, :, :]).then_inc(s["rows_scr_in"], 16)
            sp.wait_ge(s["rows_scr_in"], 32)
            for p in range(PARTS):
                for b in range(B):
                    sp.dma_start(KP[KROWS + p:KROWS + p + 1, :, b * P:(b + 1) * P],
                                 b_scr[p:p + 1, None, :].broadcast_to([1, H, P])).then_inc(s["kp_in"], 16)
                    sp.dma_start(KP[KROWS + PARTS + p:KROWS + PARTS + p + 1, :, b * P:(b + 1) * P],
                                 m_scr[b, p:p + 1, None, :].broadcast_to([1, H, P])).then_inc(s["kp_in"], 16)
            sp.wait_ge(s["zero_tile"], 1)
            sp.dma_start(x_slots.rearrange("(j p) d -> p j d", p=P),
                         ZERO[:, None, :].broadcast_to([P, NBLK, D])).then_inc(s["slots_zero"], 16)
            for p in range(PARTS):
                sp.wait_ge(s["misc_done"], p + 1)
                sp.dma_start(k_scr[p], KTP[:, p, :]).then_inc(s["k_scr_in"], 16)
            sp.wait_ge(s["k_scr_in"], 16 * PARTS)
            for i in range(PARTS):
                for j in range(PARTS):
                    r = (i * PARTS + j) * XH
                    sp.dma_start(KP[r:r + XH, :, :], k_scr[j].rearrange("(h d) q -> d h q", d=XH)).then_inc(s["kp_in"], 16)
            sp.wait_ge(s["consts"], 2)
            sp.dma_start(QP[KROWS:KALL, :, :].rearrange("r h (b q) -> r (h b) q", q=P),
                         ONES[0:KALL - KROWS, None, :].broadcast_to([KALL - KROWS, H * B, P])).then_inc(s["q_ones"], 16)
            for b in range(B):
                sp.wait_ge(s["misc_done"], PARTS + b + 1)
                sp.dma_start(q_scr[b], QT[:, b % 2, :, :]).then_inc(q_scr_in[b], 16)
                sp.wait_ge(q_scr_in[b], 16)
                for i in range(PARTS):
                    for j in range(PARTS):
                        r = (i * PARTS + j) * XH
                        sp.dma_start(QP[r:r + XH, :, b * P:(b + 1) * P],
                                     q_scr[b].rearrange("(h d) p q -> p d h q", d=XH)[i]).then_inc(q_in[b], 16)
                if b == 5:
                    sp.wait_ge(s["t_full"], NT)
                    sp.dma_start(GRAW[:, :, :], gate_w.rearrange("e (c p) h -> p (e c) h", p=P)).then_inc(s["gate_in"], 16)
                    sp.dma_start(URAW[:, :, :], up_w.rearrange("e (c p) h -> p (e c) h", p=P)).then_inc(s["up_in"], 16)
            sp.wait_ge(s["v_full"], NS)
            sp.dma_start(DRAW[:, :, :, :], down_w.rearrange("e h (c i) -> h e c i", c=2)).then_inc(s["down_in"], 16)
            sp.wait_ge(s["x_scattered"], 16 * 2 * B)
            for j in range(NBLK + 4):
                if j < NBLK:
                    if j >= 4:
                        sp.wait_ge(s["xgt_full"], j - 3)
                    sp.dma_start(XG[:, j % 4, :], x_slots[j * P:(j + 1) * P, :]).then_inc(xg_in[j % 4], 16)
                if j >= 4:
                    sp.wait_ge(s["y_done"], j - 3)
                    sp.dma_start(y_slots[(j - 4) * P:(j - 3) * P, :], YS[:, (j - 4) % 4, :]).then_inc(y_out[(j - 4) % 4], 16)
            for b in range(B):
                sp.wait_ge(s["out_ready"], b + 1)
                sp.dma_start(out[b], OUT[:, b, :]).then_inc(s["stored"], 16)
            sp.wait_ge(s["stored"], 16 * B)

        @block.gpsimd
        def _(pool):
            g = nc.gpsimd
            chain = [0]

            def link(ins):
                chain[0] += 1
                ins.then_inc(s["split_q"], 1)
                pool.wait_ge(s["split_q"], chain[0])

            link(g.memset(ID[:, :], 0.0))
            g.affine_select(out=ID[:, :], in_=ID[:, :], compare_op=ALU.not_equal, fill=1.0, base=0,
                            pattern=[[-1, P]], channel_multiplier=1).then_inc(s["ident"], 1)
            g.memset(HALF[:, :], -0.5)
            g.memset(ZERO[:, :], 0.0).then_inc(s["zero_tile"], 1)
            g.memset(WQBD[:, :, :, :], 0.0).then_inc(s["zeroed"], 1)
            g.memset(WOBD[:, :, :, :], 0.0).then_inc(s["zeroed"], 1)
            pool.wait_ge(s["ident"], 1)
            g.tensor_copy(IDB[:, :], ID[:, :]).then_inc(s["ident"], 1)
            pool.wait_ge(s["stats_x"], 1)
            pool.wait_ge(s["ident"], 2)
            g.tensor_tensor(RS[:, :], VE[:, :], HALF[:, :], ALU.pow).then_inc(s["rstd_x"], 1)
            pool.wait_ge(s["rows_in"], 32)
            link(g.iota(KIX[:, :], pattern=[[1, P]], base=0, channel_multiplier=0,
                        allow_small_or_imprecise_dtypes=True))
            link(g.tensor_copy(SLF[:, :], SLI[:, :]))
            for p, c in enumerate(mask_parts()):
                link(g.tensor_scalar(MPT[:, p, :], KIX[:, :], SLF[:, 0:1], c, ALU.is_ge, ALU.mult))
            link(g.tensor_copy(BPT[:, 0, :], BROW[:, :]))
            link(g.tensor_tensor(BRES[:, :], BROW[:, :], BPT[:, 0, :], ALU.subtract))
            link(g.tensor_copy(BPT[:, 1, :], BRES[:, :]))
            link(g.tensor_tensor(BRES[:, :], BRES[:, :], BPT[:, 1, :], ALU.subtract))
            g.tensor_copy(BPT[:, 2, :], BRES[:, :]).then_inc(s["rows_ready"], 1)
            pool.wait_ge(s["ck_in"], 16)
            for p in range(PARTS):
                src = CK if p == 0 else CKR
                link(g.tensor_copy(CKP[:, p, :, :], src[:, :, :]))
                if p + 1 < PARTS:
                    link(g.tensor_tensor(CKR[:, :, :], src[:, :, :], CKP[:, p, :, :], ALU.subtract))
            g.memset(UT[:, :], 1.0).then_inc(s["ck_parts"], 1)
            pool.wait_ge(s["ck_parts"], 1)
            g.affine_select(out=UT[:, :], in_=UT[:, :], compare_op=ALU.is_gt, fill=0.0, base=0,
                            pattern=[[1, P]], channel_multiplier=-1).then_inc(s["consts"], 1)
            g.memset(ONES[:, :], 1.0).then_inc(s["consts"], 1)

            for n in range(NU + TAIL + 4):
                if n < NU:
                    pool.wait_ge(s["sum_recip"], n + 1)
                    e = EX[:, n % 3, :].rearrange("q (h k) -> q h k", h=HU)
                    g.tensor_tensor(e, e, RCP[:, n % 4, :, None].broadcast_to([P, HU, P]), ALU.mult).then_inc(s["p_norm"], 1)
                bi, at_ = divmod(n - TAIL - 1, 4)
                if at_ == 0 and 0 <= bi < 2 * B:
                    pool.wait_ge(s["var_ready"], bi + 1)
                    g.tensor_tensor(TRS[:, bi % 2:bi % 2 + 1], TVE[:, bi % 2:bi % 2 + 1], HALF[:, 0:1],
                                    ALU.pow).then_inc(s["rstd_ready"], 1)
                bi, at_ = divmod(n - TAIL - 2, 4)
                if at_ == 0 and 0 <= bi < B:
                    pool.wait_ge(s["x_normed"], bi + 1)
                    if bi:
                        pool.wait_ge(s["misc_full"], PARTS + bi)
                    link(g.tensor_scalar(QR[:, :], X1[:, bi, :], float(XH) ** -0.5, 1.0, ALU.mult, ALU.mult))
                    for p in range(PARTS):
                        if p + 1 < PARTS:
                            link(g.tensor_copy(QB[:, p, :], QR[:, :]))
                            link(g.tensor_tensor(QR[:, :], QR[:, :], QB[:, p, :], ALU.subtract))
                        else:
                            g.tensor_copy(QB[:, p, :], QR[:, :]).then_inc(s["parts_ready"], 1)
                            pool.wait_ge(s["parts_ready"], bi + 1)
                if n == 26:
                    g.memset(VPAD[:, :, :, :], 0.0).then_inc(s["vpad_zero"], 1)
                if n >= NS - 1 and n < NU and (n - NS + 1) % UB == 0:
                    b = (n - NS + 1) // UB
                    if b < B:
                        pool.wait_ge(s["cv_in"], 16)
                        pool.wait_ge(s["vpad_zero"], 1)
                        if b >= 2:
                            pool.wait_ge(s["pv_full"], NS + UB * (b - 1))
                        diag = VPAD[:, b % 2, :, :].rearrange("k h n -> k (h n)")
                        dst = bass.AP(diag.tensor, diag.offset, [list(diag.ap[0]), [D + XH, H], [1, XH]])
                        g.tensor_copy(dst, CV[:, b, :].rearrange("k (h d) -> k h d", h=H)).then_inc(s["vpad_done"], 1)
            pool.wait_ge(s["misc_done"], PARTS + 2 * B)
            kw = dict(channel_multiplier=0, allow_small_or_imprecise_dtypes=True)
            g.iota(WTE[:, :, :], pattern=[[0, B], [-1, E]], base=E, **kw).then_inc(s["consts"], 1)
            g.iota(THR[:, :, :], pattern=[[0, E], [P, 8]], base=0, **kw).then_inc(s["consts"], 1)
            g.iota(BLK[:, :, :], pattern=[[1, NBLK + 1], [0, E]], base=0, **kw).then_inc(s["consts"], 1)
            link(g.memset(TRI[:, :, :], 1.0))
            g.affine_select(out=TRI[:, :, :], in_=TRI[:, :, :], compare_op=ALU.is_ge, fill=0.0, base=0,
                            pattern=[[1, E], [-1, E]], channel_multiplier=0).then_inc(s["consts"], 1)
            pool.wait_ge(s["slots_zero"], 16)
            pool.wait_ge(s["slots_ready"], 1)
            for b in range(B):
                for k in range(2):
                    g.indirect_dma_start(out=x_slots, out_offset=bass.IndirectOffsetOnAxis(ap=SLOT[:, k, b:b + 1], axis=0),
                                         in_=X2[:, b, :], in_offset=None).then_inc(s["x_scattered"], 16)
            for i in range(4):
                pool.wait_ge(y_out[i], 16 * len(range(i, NBLK, 4)))
            for b in range(B):
                for k, dst in enumerate((G1, G2)):
                    g.indirect_dma_start(out=dst[:, b, :], out_offset=None, in_=y_slots,
                                         in_offset=bass.IndirectOffsetOnAxis(ap=SLOT[:, k, b:b + 1], axis=0)).then_inc(s["gathered"], 16)
            pool.wait_ge(s["last_var"], 1)
            g.tensor_tensor(RS[:, :], VE[:, :], HALF[:, :], ALU.pow).then_inc(s["last_rstd"], 1)

        @block.scalar
        def _(act):
            a = nc.scalar
            act.dma_start(WK[:, :], wk).then_inc(s["wk_in"], 16)
            act.dma_start(GB_[:, 0:1], gamma.rearrange("(d a) -> d a", a=1)).then_inc(s["gb_in"], 16)
            act.dma_start(GB_[:, 1:2], beta.rearrange("(d a) -> d a", a=1)).then_inc(s["gb_in"], 16)
            act.dma_start(RW[:, :], router_w.rearrange("e h -> h e"),
                          allow_slow_non_contiguous=True).then_inc(s["rw_in"], 16)

            def setup(i, out_ap, then):
                act.wait_ge(s["setup_full"], i + 1)
                a.activation(out_ap, sbank(i)[:, :], ACT.Copy).then_inc(then, 1)

            for i in range(2):
                setup(K0 + i, WKT[:, 4 * i:4 * i + 4, :], set_done[K0 + i])
            for i in range(2):
                act.wait_ge(s["xtf_done"], i + 1)
                a.activation(XTh[:, 512 * i:512 * i + 512], XTF[:, 512 * i:512 * i + 512], ACT.Copy).then_inc(s["xth_done"], 1)
            for i in range(4):
                setup(M0 + i, Mh[:, 4 * i:4 * i + 4, :], s["mh_done"])
            for i in range(2):
                setup(WV0 + i, WVT[:, 4 * i:4 * i + 4, :], set_done[WV0 + i])
            for i in range(4):
                setup(O0 + i, Vh[:, 4 * i:4 * i + 4, :], s["oh_done"])

            def t_high(t):
                grp, pair = divmod(t, TLEAD)
                act.wait_ge(s["t_full"], t + 1)
                b_ = bank[t % 2] if t < TLEAD else bank[T_BANK]
                a.activation(Th[:, grp % 2, :, 2 * pair:2 * pair + 2, :].rearrange("d b h k -> d h b k"),
                             b_[:, :].rearrange("d (h b k) -> d h b k", h=2, b=GB), ACT.Copy).then_inc(s["th_done"], 1)

            for t in range(TLEAD):
                t_high(t)
            for n in range(NU + TAIL + 4):
                if n + TLEAD < NT:
                    t_high(n + TLEAD)
                if n < NU:
                    act.wait_ge(s["max_done"], n + 1)
                    if n >= 3:
                        act.wait_ge(s["pt_full"], n - 2)
                    if n == 0:
                        act.wait_ge(s["setup_full"], N_SETUP)
                    for j in range(HU):
                        ins = a.activation(EX[:, n % 3, j * P:(j + 1) * P], bank[S_BANK[n % 2]][:, j * P:(j + 1) * P],
                                           ACT.Exp, bias=NMX[:, n % 4, j:j + 1], accum_out=SUM[:, n % 4, j:j + 1])
                    ins.then_inc(s["exp_done"], 1)
                k = n - PT_LAG
                if 0 <= k < NS:
                    act.wait_ge(s["v_full"], k + 1)
                    if k >= 3:
                        act.wait_ge(s["pv_full"], k - 2)
                    a.activation(VP[:, k % 3, :], bank[V_BANK][:, :], ACT.Copy).then_inc(s["v_done"], 1)
                w = n - NS - 2
                if 0 <= w < 8:
                    act.wait_ge(s["w_full"], w + 1)
                    e2 = 2 * (w % 4)
                    a.activation(WGUh[:, e2:e2 + 2, w // 4, :], bank[T_BANK][:, :].rearrange("h (e i) -> h e i", e=2),
                                 ACT.Copy).then_inc(s["wh_done"], 1)
                if 8 <= w < 12:
                    act.wait_ge(s["w_full"], w + 1)
                    e2 = 2 * (w - 8)
                    a.activation(WD[:, e2:e2 + 2, :, :], bank[T_BANK][:, :].rearrange("i (e c h) -> i e c h", e=2, c=2),
                                 ACT.Copy).then_inc(s["w_done"], 1)
                if 3 <= n < 3 + PARTS:
                    p = n - 3
                    act.wait_ge(s["misc_full"], p + 1)
                    a.activation(KTP[:, p, :], bank[MISC][:, :].bitcast(BF16), ACT.Copy).then_inc(s["misc_done"], 1)
                bi, at_ = divmod(n - TAIL - 3, 4)
                if at_ == 0 and 0 <= bi < B:
                    act.wait_ge(s["misc_full"], PARTS + bi + 1)
                    if bi >= 2:
                        act.wait_ge(q_scr_in[bi - 2], 16)
                    a.activation(QT[:, bi % 2, :, :].rearrange("d p q -> d (p q)"),
                                 bank[MISC][:, :].bitcast(BF16)[:, 0:PARTS * P], ACT.Copy).then_inc(s["misc_done"], 1)
                if at_ == 0 and B <= bi < 2 * B:
                    act.wait_ge(s["misc_full"], PARTS + bi + 1)
                    if bi > B:
                        act.wait_ge(s["router_full"], bi - B)
                    a.activation(X2T[:, :], bank[MISC][:, 0:P], ACT.Copy).then_inc(s["misc_done"], 1)
            act.wait_ge(s["route_l"], 1)
            a.activation(PE_[:, :, :], LG[:, :, :], ACT.Exp).then_inc(s["route_exp"], 1)
            for j in range(NBLK + 2):
                if j < NBLK:
                    act.wait_ge(s["xgt_full"], j + 1)
                    if j >= 2:
                        act.wait_ge(s["gu_full"], j - 1)
                    a.activation(XGTh[:, j % 2, :], bank[S_BANK[j % 2]][:, 0:P], ACT.Copy).then_inc(s["xgh_done"], 1)
                k = j - 1
                if 0 <= k < NBLK:
                    act.wait_ge(s["gu_full"], k + 1)
                    if k >= 2:
                        act.wait_ge(s["hu_done"], k - 1)
                    a.activation(SG[:, k % 2, :], bank[PT_BANK[k % 2]][:, 0:FI], ACT.Silu).then_inc(s["silu_done"], 1)
                k = j - 2
                if 0 <= k < NBLK:
                    act.wait_ge(s["ht_full"], k + 1)
                    if k >= 2:
                        act.wait_ge(s["dn_full"], k - 1)
                    a.activation(HT[:, k % 2, :, :].rearrange("i c t -> i (c t)"), bank[6 + k % 2][:, 0:FI],
                                 ACT.Copy).then_inc(s["ht_done"], 1)

        @block.vector
        def _(dve):
            v = nc.vector
            chain = [0]

            def link(ins):
                chain[0] += 1
                ins.then_inc(s["chain"], 1)
                dve.wait_ge(s["chain"], chain[0])

            dve.wait_ge(s["x_in"], 16)
            for b in range(B):
                ins = v.bn_stats(BST[:, b, :], X[:, b, :])
            link(ins)
            for b in range(B):
                ins = v.bn_aggr(BMV[:, b, :], BST[:, b, :])
            link(ins)
            v.tensor_scalar(VE[:, :], BMV[:, :, 1], EPS, None, ALU.add).then_inc(s["stats_x"], 1)
            dve.wait_ge(s["zeroed"], 1)

            def wq_half(i):
                dve.wait_ge(s["setup_full"], Q0 + i + 1)
                for j in range(2):
                    ins = v.tensor_scalar(WQBD[DH * j:DH * j + DH, 4 * i:4 * i + 4, j, :],
                                          sbank(Q0 + i)[DH * j:DH * j + DH, :].rearrange("p (c d) -> p c d", c=4),
                                          float(DH) ** -0.5, None, ALU.mult)
                ins.then_inc(set_done[Q0 + i], 1)

            dve.wait_ge(s["rstd_x"], 1)
            for b in range(B):
                v.tensor_scalar(XHAT[:, b, :], X[:, b, :], BMV[:, b, 0:1], RS[:, b:b + 1], ALU.subtract,
                                ALU.mult).then_inc(s["xhat_done"], 1)
            for i in range(2):
                wq_half(i)
            dve.wait_ge(s["gb_in"], 32)
            for i in range(2):
                c = slice(512 * i, 512 * i + 512)
                dve.wait_ge(s["setup_full"], X0 + i + 1)
                v.tensor_scalar(XTF[:, c], sbank(X0 + i)[:, :], GB_[:, 0:1], GB_[:, 1:2], ALU.mult,
                                ALU.add).then_inc(s["xtf_done"], 1)
                dve.wait_ge(s["xtf_done"], i + 1)
            for i in range(2):
                c = slice(512 * i, 512 * i + 512)
                dve.wait_ge(s["xth_done"], i + 1)
                v.tensor_tensor(XTl[:, c], XTF[:, c], XTh[:, c].bitcast(F32), ALU.subtract).then_inc(s["xtl_done"], 1)

            def low(i, high, low_, done):
                dve.wait_ge(done[0], done[1])
                hs = slice(4 * (i % 4), 4 * (i % 4) + 4)
                return v.tensor_tensor(low_[:, hs, :], sbank(done[2])[:, :].rearrange("p (h d) -> p h d", h=4),
                                       high[:, hs, :].bitcast(F32), ALU.subtract)

            for i in range(4):
                low(i, Mh, Ml, (s["mh_done"], i + 1, M0 + i)).then_inc(set_done[M0 + i], 1)
            for i in range(4):
                low(i, Vh, Vl, (s["oh_done"], i + 1, O0 + i)).then_inc(set_done[O0 + i], 1)

            def t_low(t):
                grp, pair = divmod(t, TLEAD)
                dve.wait_ge(s["th_done"], t + 1)
                b_ = bank[t % 2] if t < TLEAD else bank[T_BANK]
                to = lambda T: T[:, grp % 2, :, 2 * pair:2 * pair + 2, :].rearrange("d b h k -> d h b k")
                v.tensor_tensor(to(Tl), b_[:, :].rearrange("d (h b k) -> d h b k", h=2, b=GB), to(Th).bitcast(F32),
                                ALU.subtract).then_inc(s["tl_done"], 1)

            for t in range(TLEAD):
                t_low(t)
            for n in range(NU + TAIL + 4):
                if n + TLEAD < NT:
                    t_low(n + TLEAD)
                if n < NU:
                    dve.wait_ge(s["s_full"], n + 1)
                    v.tensor_reduce(NMX[:, n % 4, :], bank[S_BANK[n % 2]][:, :].rearrange("q (h k) -> q h k", h=HU),
                                    axis=AX_X, op=ALU.max, negate=True).then_inc(s["max_done"], 1)
                k = n - PT_LAG
                if 0 <= k < NU:
                    dve.wait_ge(s["pt_full"], k + 1)
                    if k >= 3:
                        dve.wait_ge(s["pv_full"], k - 2)
                    v.tensor_copy(PTs[:, k % 3, :], bank[PT_BANK[k % 2]][:, :]).then_inc(s["pt_done"], 1)
                if n < NU:
                    dve.wait_ge(s["exp_done"], n + 1)
                    v.reciprocal(RCP[:, n % 4, :], SUM[:, n % 4, :]).then_inc(s["sum_recip"], 1)
                w = n - NS - 2
                if 0 <= w < 8:
                    dve.wait_ge(s["wh_done"], w + 1)
                    e2 = 2 * (w % 4)
                    v.tensor_tensor(WGUl[:, e2:e2 + 2, w // 4, :], bank[T_BANK][:, :].rearrange("h (e i) -> h e i", e=2),
                                    WGUh[:, e2:e2 + 2, w // 4, :].bitcast(F32), ALU.subtract).then_inc(s["w_done"], 1)
                bi, at_ = divmod(n - TAIL, 4)
                if at_ == 0 and 0 <= bi < 2 * B:
                    dve.wait_ge(s["pv_full"], UB * bi + UB)
                    v.tensor_tensor(Y[:, bi % 2, :], bank[ACC][:, 0:D], (X if bi < B else X1)[:, bi % B, :],
                                    ALU.add).then_inc(s["y_added"], 1)
                if at_ == 1 and 0 <= bi < 2 * B:
                    dve.wait_ge(s["y_added"], bi + 1)
                    link(v.bn_stats(TST[:, :], Y[:, bi % 2, :]))
                    link(v.bn_aggr(TMV[:, bi % 2, :], TST[:, :]))
                    v.tensor_scalar(TVE[:, bi % 2:bi % 2 + 1], TMV[:, bi % 2, 1:2], EPS, None, ALU.add).then_inc(s["var_ready"], 1)
                if at_ == 2 and 0 <= bi < 2 * B:
                    dve.wait_ge(s["rstd_ready"], bi + 1)
                    v.tensor_scalar((X1 if bi < B else X2)[:, bi % B, :], Y[:, bi % 2, :], TMV[:, bi % 2, 0:1],
                                    TRS[:, bi % 2:bi % 2 + 1], ALU.subtract, ALU.mult).then_inc(s["x_normed"], 1)

            dve.wait_ge(s["router_full"], B)
            lg = bank[V_BANK][:, 0:B * E].rearrange("p (b e) -> p b e", b=B)
            row = lambda i: ROWS[:, i, :]
            wide = lambda i: ROWS[:, i, :, None].broadcast_to([P, B, E])
            link(v.tensor_reduce(row(0), lg, axis=AX_X, op=ALU.max))
            v.tensor_tensor(LG[:, :, :], lg, wide(0), ALU.subtract).then_inc(s["route_l"], 1)
            dve.wait_ge(s["route_exp"], 1)
            link(v.tensor_reduce(row(1), PE_[:, :, :], axis=AX_X, op=ALU.add))
            link(v.reciprocal(row(2), row(1)))
            link(v.tensor_tensor(PE_[:, :, :], PE_[:, :, :], wide(2), ALU.mult))
            dve.wait_ge(s["consts"], 6)
            for k, hot in enumerate((OH1, OH2)):
                link(v.tensor_reduce(row(3 + k), PE_[:, :, :], axis=AX_X, op=ALU.max))
                link(v.tensor_tensor(EQ[:, :, :], PE_[:, :, :], wide(3 + k), ALU.is_equal))
                link(v.tensor_tensor(EQ[:, :, :], EQ[:, :, :], WTE[:, :, :], ALU.mult))
                link(v.tensor_reduce(row(5), EQ[:, :, :], axis=AX_X, op=ALU.max))
                link(v.tensor_tensor(hot[:, :, :], EQ[:, :, :], wide(5), ALU.is_equal))
                if k == 0:
                    link(v.scalar_tensor_tensor(PE_[:, :, :], hot[:, :, :], -2.0, PE_[:, :, :], ALU.mult, ALU.add))
            v.tensor_tensor(AB[:, :, :], OH1[:, :, :], OH2[:, :, :], ALU.add).then_inc(s["a_ready"], 1)
            link(v.tensor_tensor(row(6), row(3), row(4), ALU.add))
            link(v.reciprocal(row(7), row(6)))
            for k in range(2):
                link(v.tensor_tensor(row(8 + k), row(3 + k), row(7), ALU.mult))
            dve.wait_ge(s["rank_full"], 1)
            cnt = bank[S_BANK[1]][:, 0:E]
            link(v.tensor_copy(CNT[:, 0, :], cnt))
            link(v.tensor_tensor(CMP[:, 0:E, :], CNT[:, 0, :, None].broadcast_to([P, E, 8]), THR[:, :, :], ALU.is_gt))
            link(v.tensor_reduce(CNT[:, 1, :], CMP[:, 0:E, :], axis=AX_X, op=ALU.add))
            link(v.tensor_tensor(CMP[:, 0:E, :], CNT[:, 1, None, :].broadcast_to([P, E, E]), TRI[:, :, :], ALU.mult))
            link(v.tensor_reduce(CNT[:, 2, :], CMP[:, 0:E, :], axis=AX_X, op=ALU.add))
            link(v.tensor_tensor(CNT[:, 3, :], CNT[:, 2, :], CNT[:, 1, :], ALU.subtract))
            link(v.scalar_tensor_tensor(SL[:, :, :], CNT[:, 3, None, :].broadcast_to([P, B, E]), float(P),
                                        bank[S_BANK[0]][:, 0:B * E].rearrange("p (b e) -> p b e", b=B), ALU.mult, ALU.add))
            for k, hot in enumerate((OH1, OH2)):
                link(v.tensor_tensor(EQ[:, :, :], hot[:, :, :], SL[:, :, :], ALU.mult))
                link(v.tensor_reduce(row(10 + k), EQ[:, :, :], axis=AX_X, op=ALU.add))
            v.tensor_copy(SLOT[:, :, :], ROWS[:, 10:12, :]).then_inc(s["slots_ready"], 1)
            link(v.tensor_tensor(CMP[:, :, :], CNT[:, 2, None, :].broadcast_to([P, NBLK + 1, E]), BLK[:, :, :], ALU.is_le))
            link(v.tensor_reduce(EIDF[:, :], CMP[:, :, :], axis=AX_X, op=ALU.add))
            v.tensor_scalar(EID[:, :], EIDF[:, :], float(E - 1), None, ALU.min).then_inc(s["eid_ready"], 1)
            for j in range(NBLK + 3):
                if j < NBLK:
                    dve.wait_ge(s["xgh_done"], j + 1)
                    v.tensor_tensor(XGTl[:, j % 2, :], bank[S_BANK[j % 2]][:, 0:P], XGTh[:, j % 2, :].bitcast(F32),
                                    ALU.subtract).then_inc(s["xgl_done"], 1)
                k = j - 1
                if 0 <= k < NBLK:
                    dve.wait_ge(s["silu_done"], k + 1)
                    if k >= 2:
                        dve.wait_ge(s["ht_full"], k - 1)
                    v.tensor_tensor(HUs[:, k % 2, :], bank[PT_BANK[k % 2]][:, FI:2 * FI], SG[:, k % 2, :],
                                    ALU.mult).then_inc(s["hu_done"], 1)
                k = j - 3
                if 0 <= k < NBLK:
                    dve.wait_ge(s["dn_full"], k + 1)
                    if k >= 4:
                        dve.wait_ge(y_out[k % 4], 16 * (k // 4))
                    v.tensor_copy(YS[:, k % 4, :], bank[k % 2][:, 0:D]).then_inc(s["y_done"], 1)
            dve.wait_ge(s["gathered"], 16 * 2 * B)
            for b in range(B):
                v.scalar_tensor_tensor(Z[:, b, :], G1[:, b, :], ROWS[:, 8, b:b + 1], X2[:, b, :], ALU.mult,
                                       ALU.add).then_inc(s["z_done"], 1)
            for b in range(B):
                dve.wait_ge(s["z_done"], b + 1)
                v.scalar_tensor_tensor(Z[:, b, :], G2[:, b, :], ROWS[:, 9, b:b + 1], Z[:, b, :], ALU.mult,
                                       ALU.add).then_inc(s["z_done"], 1)
            for b in range(B):
                dve.wait_ge(s["z_done"], B + b + 1)
                ins = v.bn_stats(BST[:, b, :], Z[:, b, :])
            link(ins)
            for b in range(B):
                ins = v.bn_aggr(BMV[:, b, :], BST[:, b, :])
            link(ins)
            v.tensor_scalar(VE[:, :], BMV[:, :, 1], EPS, None, ALU.add).then_inc(s["last_var"], 1)
            dve.wait_ge(s["last_rstd"], 1)
            for b in range(B):
                v.tensor_scalar(OUT[:, b, :], Z[:, b, :], BMV[:, b, 0:1], RS[:, b:b + 1], ALU.subtract,
                                ALU.mult).then_inc(s["out_ready"], 1)

        @block.tensor
        def _(pe):
            mm = nc.tensor.matmul

            def split_mm(out_ap, ah, al, bh, bl):
                mm(out_ap, ah, bh, start=True, stop=False)
                mm(out_ap, ah, bl, start=False, stop=False)
                return mm(out_ap, al, bh, start=False, stop=True)

            pe.wait_ge(s["ident"], 1)

            def room(i):
                if i >= 4:
                    j = i - 4
                    if X0 <= j < X0 + 2:
                        pe.wait_ge(s["xtf_done"], j - X0 + 1)
                    else:
                        pe.wait_ge(set_done[j], 1)

            def transposes(i, src):
                room(i)
                for j in range(4):
                    ins = nc.tensor.transpose(sbank(i)[:, j * P:(j + 1) * P], src(j), ID[:, :])
                ins.then_inc(s["setup_full"], 1)

            pe.wait_ge(s["wk_in"], 16)
            for i in range(2):
                transposes(K0 + i, lambda j: WK[:, (4 * i + j) * P:(4 * i + j + 1) * P])
            pe.wait_ge(s["wq_in"], 16)
            for i in range(2):
                transposes(Q0 + i, lambda j: WQ[:, (4 * i + j) * P:(4 * i + j + 1) * P])
            for i in range(2):
                pe.wait_ge(s["xhat_done"], 4 * i + 4)
                transposes(X0 + i, lambda j: XHAT[:, 4 * i + j, :])

            def weight_products(i0, wt, bd):
                for i in range(4):
                    room(i0 + i)
                    for j in range(2):
                        c = 2 * i + j
                        ins = mm(sbank(i0 + i)[:, 2 * D * j:2 * D * (j + 1)], wt[:, c, :],
                                 bd[:, c, :, :].rearrange("p j d -> p (j d)"), start=True, stop=True)
                    ins.then_inc(s["setup_full"], 1)

            for i in (K0, K0 + 1, Q0, Q0 + 1):
                pe.wait_ge(set_done[i], 1)
            weight_products(M0, WKT, WQBD)
            pe.wait_ge(s["wv_in"], 16)
            for i in range(2):
                transposes(WV0 + i, lambda j: WV[:, (4 * i + j) * P:(4 * i + j + 1) * P])
            pe.wait_ge(s["wo_in"], 32)
            for i in range(2):
                pe.wait_ge(set_done[WV0 + i], 1)
            weight_products(O0, WVT, WOBD)

            def t_product(t):
                grp, pair = divmod(t, TLEAD)
                if t < TLEAD:
                    b_ = bank[t % 2]
                    pe.wait_ge(s["xtl_done"], 1)
                    pe.wait_ge(set_done[M0 + pair // 2], 1)
                    if t >= 2:
                        pe.wait_ge(s["tl_done"], t - 1)
                else:
                    b_ = bank[T_BANK]
                    pe.wait_ge(s["xtl_done"], grp // 2 + 1)
                    pe.wait_ge(s["tl_done"], t)
                c = slice(grp * GB * P, (grp + 1) * GB * P)
                for j in range(2):
                    h = 2 * pair + j
                    ins = split_mm(b_[:, GB * P * j:GB * P * (j + 1)], Mh[:, h, :], Ml[:, h, :], XTh[:, c], XTl[:, c])
                ins.then_inc(s["t_full"], 1)

            for t in range(TLEAD):
                t_product(t)
            for n in range(NU + TAIL + 5):
                if n + TLEAD < NT:
                    t_product(n + TLEAD)
                b, u = unit(n)
                c = slice(b * P, (b + 1) * P)
                if n < NU:
                    if n < 2:
                        pe.wait_ge(set_done[12 + n], 1)
                    else:
                        pe.wait_ge(s["exp_done"], n - 1)
                    sb_ = bank[S_BANK[n % 2]]
                if n < NS:
                    grp = b // GB
                    pe.wait_ge(s["tl_done"], TLEAD * grp + 2 * u + 2)
                    t_of = lambda T: T[:, grp % 2, b % GB, HU * u:HU * u + HU, :].rearrange("d h k -> d (h k)")
                    split_mm(sb_[:, :], XTh[:, c], XTl[:, c], t_of(Th), t_of(Tl)).then_inc(s["s_full"], 1)
                elif n < NU:
                    pe.wait_ge(s["kp_in"], 16 * (2 * PARTS * B + PARTS * PARTS))
                    pe.wait_ge(s["q_ones"], 16)
                    pe.wait_ge(q_in[b], 16 * PARTS * PARTS)
                    for j in range(HU):
                        h = HU * u + j
                        ins = mm(sb_[:, j * P:(j + 1) * P], QP[0:KALL, h, c], KP[0:KALL, h, c], start=True, stop=True)
                    ins.then_inc(s["s_full"], 1)
                k = n - PT_LAG
                if 0 <= k < NS:
                    kb, ku = unit(k)
                    if k == 0:
                        pe.wait_ge(s["tl_done"], TLEAD)
                    else:
                        pe.wait_ge(s["v_done"], k)
                    pe.wait_ge(set_done[O0 + ku], 1)
                    kc = slice(kb * P, (kb + 1) * P)
                    v_of = lambda V: V[:, HU * ku:HU * ku + HU, :].rearrange("d h n -> d (h n)")
                    split_mm(bank[V_BANK][:, :], XTh[:, kc], XTl[:, kc], v_of(Vh), v_of(Vl)).then_inc(s["v_full"], 1)
                if 0 <= k < NU:
                    pe.wait_ge(s["p_norm"], k + 1)
                    if k < 2:
                        pe.wait_ge(set_done[14 + k], 1)
                    else:
                        pe.wait_ge(s["pt_done"], k - 1)
                    for j in range(HU):
                        ins = nc.tensor.transpose(bank[PT_BANK[k % 2]][:, j * P:(j + 1) * P],
                                                  EX[:, k % 3, j * P:(j + 1) * P], ID[:, :])
                    ins.then_inc(s["pt_full"], 1)
                k = n - PV_LAG
                if 0 <= k < NU:
                    kb, ku = unit(k)
                    bi = k // UB
                    pe.wait_ge(s["pt_done"], k + 1)
                    if k < NS:
                        pe.wait_ge(s["v_done"], k + 1)
                    else:
                        pe.wait_ge(s["vpad_done"], kb + 1)
                    if ku == 0 and bi:
                        pe.wait_ge(s["y_added"], bi)
                    for j in range(HU):
                        vals = VP[:, k % 3, j * D:(j + 1) * D] if k < NS else VPAD[:, kb % 2, HU * ku + j, :]
                        ins = mm(bank[ACC][:, 0:D], PTs[:, k % 3, j * P:(j + 1) * P], vals,
                                 start=ku == 0 and j == 0, stop=ku == UB - 1 and j == HU - 1)
                    ins.then_inc(s["pv_full"], 1)
                w = n - NS - 2
                if 0 <= w < 12:
                    if w == 0:
                        pe.wait_ge(s["tl_done"], NT)
                    else:
                        pe.wait_ge(s["w_done"], w)
                    pe.wait_ge(s[("gate_in", "up_in", "down_in")[w // 4]], 16)
                    for j in range(4):
                        if w < 8:
                            src = (GRAW if w < 4 else URAW)[:, 4 * (w % 4) + j, :]
                        else:
                            src = DRAW[:, 2 * (w - 8) + j // 2, j % 2, :]
                        ins = nc.tensor.transpose(bank[T_BANK][:, j * P:(j + 1) * P], src, ID[:, :])
                    ins.then_inc(s["w_full"], 1)
                if 3 <= n < 3 + PARTS:
                    p = n - 3
                    if p == 0:
                        pe.wait_ge(s["ck_parts"], 1)
                        pe.wait_ge(s["ident"], 2)
                    else:
                        pe.wait_ge(s["misc_done"], p)
                    for b2 in range(B):
                        ins = nc.tensor.transpose(bank[MISC][:, :].bitcast(BF16)[:, b2 * P:(b2 + 1) * P],
                                                  CKP[:, p, b2, :], IDB[:, :])
                    ins.then_inc(s["misc_full"], 1)
                bi, at_ = divmod(n - TAIL - 3, 4)
                if at_ == 0 and 0 <= bi < B:
                    pe.wait_ge(s["parts_ready"], bi + 1)
                    pe.wait_ge(s["misc_done"], PARTS + bi)
                    for p in range(PARTS):
                        ins = nc.tensor.transpose(bank[MISC][:, :].bitcast(BF16)[:, p * P:(p + 1) * P], QB[:, p, :], IDB[:, :])
                    ins.then_inc(s["misc_full"], 1)
                if at_ == 0 and B <= bi < 2 * B:
                    pe.wait_ge(s["x_normed"], bi + 1)
                    pe.wait_ge(s["misc_done"], PARTS + bi)
                    nc.tensor.transpose(bank[MISC][:, 0:P], X2[:, bi - B, :], ID[:, :]).then_inc(s["misc_full"], 1)
                if at_ == 1 and B <= bi < 2 * B:
                    e = bi - B
                    pe.wait_ge(s["misc_done"], PARTS + bi + 1)
                    if e == 0:
                        pe.wait_ge(s["rw_in"], 16)
                        pe.wait_ge(s["v_done"], NS)
                    mm(bank[V_BANK][:, e * E:(e + 1) * E], X2T[:, :], RW[:, :], start=True, stop=True).then_inc(s["router_full"], 1)
            pe.wait_ge(s["a_ready"], 1)
            rank, cnt = bank[S_BANK[0]], bank[S_BANK[1]]
            mm(rank[:, 0:B * E], UT[:, :], AB[:, :, :].rearrange("p b e -> p (b e)"), start=True, stop=False)
            for b in range(B - 1):
                mm(rank[:, (b + 1) * E:B * E].rearrange("p (b e) -> p b e", e=E), ONES[:, :],
                   AB[:, b:b + 1, :].broadcast_to([P, B - 1 - b, E]), start=False, stop=b == B - 2)
            for b in range(B):
                ins = mm(cnt[:, 0:E], ONES[:, :], AB[:, b, :], start=b == 0, stop=b == B - 1)
            ins.then_inc(s["rank_full"], 1)

            pe.wait_ge(s["eid_ready"], 1)
            expert = {}
            for j in range(NBLK + 3):
                if j < NBLK:
                    pe.wait_ge(xg_in[j % 4], 16 * (j // 4 + 1))
                    if j >= 2:
                        pe.wait_ge(s["xgl_done"], j - 1)
                    nc.tensor.transpose(bank[S_BANK[j % 2]][:, 0:P], XG[:, j % 4, :], ID[:, :]).then_inc(s["xgt_full"], 1)
                k = j - 1
                if 0 <= k < NBLK:
                    expert[k] = nc.tensor.value_load(EID[0:1, k:k + 1], min_val=0, max_val=E - 1)
                    pe.wait_ge(s["xgl_done"], k + 1)
                    if k >= 2:
                        pe.wait_ge(s["hu_done"], k - 1)
                    w_of = lambda W: W[:, :, :, :].rearrange("d e g i -> d e (g i)")[:, bass.ds(expert[k], 1), :].rearrange("d e n -> d (e n)")
                    split_mm(bank[PT_BANK[k % 2]][:, :], XGTh[:, k % 2, :], XGTl[:, k % 2, :], w_of(WGUh),
                             w_of(WGUl)).then_inc(s["gu_full"], 1)
                k = j - 2
                if 0 <= k < NBLK:
                    pe.wait_ge(s["hu_done"], k + 1)
                    if k >= 2:
                        pe.wait_ge(s["ht_done"], k - 1)
                    for c in range(2):
                        ins = nc.tensor.transpose(bank[6 + k % 2][:, c * P:(c + 1) * P], HUs[:, k % 2, c * P:(c + 1) * P], ID[:, :])
                    ins.then_inc(s["ht_full"], 1)
                k = j - 3
                if 0 <= k < NBLK:
                    pe.wait_ge(s["ht_done"], k + 1)
                    if k >= 2:
                        pe.wait_ge(s["y_done"], k - 1)
                    for c in range(2):
                        rhs = WD[:, :, c, :][:, bass.ds(expert[k], 1), :].rearrange("i e h -> i (e h)")
                        ins = mm(bank[k % 2][:, 0:D], HT[:, k % 2, c, :], rhs, start=c == 0, stop=c == 1)
                    ins.then_inc(s["dn_full"], 1)


_INS = ["x", "ctx_2048", "itok_Bx1_68_817", "L0_attn_ln_gamma", "L0_attn_ln_beta", "L0_attn_Wq", "L0_attn_Wk",
        "L0_attn_Wv", "L0_attn_Wo", "L0_xattn_b", "L0_ffn_router_w", "L0_ffn_gate_w", "L0_ffn_up_w", "L0_ffn_down_w"]


def kernel(**inputs):
    import numpy as np
    import concourse.bacc as bacc
    from concourse.bass_utils import run_bass_kernel_spmd

    nc = bacc.Bacc("TRN2", target_bir_lowering=False, num_devices=1)
    arrays, args = {}, []
    for name in _INS:
        a = np.ascontiguousarray(inputs[name])
        arrays[f"in_{name}"] = a
        args.append(nc.dram_tensor(f"in_{name}", a.shape, mybir.dt.from_np(a.dtype), kind="ExternalInput").ap())
    args.append(nc.dram_tensor("out_0", (B, P, D), F32, kind="ExternalOutput").ap())
    decoder_layer(nc, *args)
    r = run_bass_kernel_spmd(nc, [arrays], core_ids=[0])
    return r.results[0]["out_0"]
```

```python
from contextlib import ExitStack

import concourse.bass as bass
from concourse import mybir

F32 = mybir.dt.float32
F32R = mybir.dt.float32r
BF16 = mybir.dt.bfloat16
F16 = mybir.dt.float16
I32 = mybir.dt.int32
ALU = mybir.AluOpType
ACT = mybir.ActivationFunctionType
AX_X = mybir.AxisListType.X
SIZE = {F32: 4, F32R: 4, BF16: 2, F16: 2, I32: 4}

P = 128
B = 8
D = 128
H = 16
DH = 64
HU = 4
UB = H // HU
NU = B * UB
GB = 2
NG = B // GB
TG = H // 2
NT = NG * TG
XH = D // H
PARTS = 3
KROWS = PARTS * PARTS * XH
KMAX = KROWS + 2 * PARTS
KALL = KMAX + PARTS
VC = PARTS * XH + 1
EPS = 1e-5
E = 8
FI = 256
NTOK = B * P
NF = NG * E

PT_LAG, PV_LAG = 2, 3
TAIL = UB - 1 + PV_LAG
XLEAD = 2 * UB
XS = NU - XLEAD
ST_LAG = XLEAD
PX_LAG = ST_LAG + 2
XTAIL = UB - 1 + PX_LAG
X2T = XTAIL + 4
ROUTE = XTAIL + 6
W0 = NU - UB
F0 = NU + UB * 2
STEPS = F0 + NF + 3
assert UB * (GB - 1) + X2T + 1 < XLEAD + 2 * (F0 - NU)


def x_items(n):
    if n < XS:
        return ()
    return (n - XS,) if n < NU else (XLEAD + 2 * (n - NU), XLEAD + 2 * (n - NU) + 1)


def mask_parts():
    import numpy as np
    rest, out = np.float32(-1e12), []
    for _ in range(PARTS):
        top = np.array([rest], np.float32).view(np.uint32) & np.uint32(0xFFFF0000)
        out.append(float(top.view(np.float32)[0]))
        rest = np.float32(rest - np.float32(out[-1]))
    assert rest == 0
    return out


def decoder_layer(nc, x_in, ctx_in, seq_len, gamma, beta, wq, wk, wv, wo, key_bias, router_w, gate_w, up_w,
                  down_w, out):
    stack = ExitStack()
    with stack:
        sem = lambda name: stack.enter_context(nc.semaphore(name))
        KB = 1024
        base = (nc.sbuf_base + 63) // 64 * 64
        ARENA = 207 * KB
        stack.enter_context(nc.sbuf_tensor("arena", [P, ARENA // 4 + 16], F32))

        def at(name, kb, shape, dt=F32):
            n = SIZE[dt]
            for size in shape[1:]:
                n *= size
            assert kb * KB + n <= ARENA, name
            return nc.alloc_sbuf_tensor_at(name, shape, dt, offset=base + int(kb * KB))

        def shelf(kb, end):
            cur = [kb * KB]

            def put(name, shape, dt=F32):
                n = SIZE[dt]
                for size in shape[1:]:
                    n *= size
                t = nc.alloc_sbuf_tensor_at(name, shape, dt, offset=base + cur[0])
                cur[0] += (n + 31) // 32 * 32
                assert cur[0] <= end * KB, name
                return t
            return put

        X = at("X", 0, [P, B, D])
        X2 = at("X2", 0, [P, B, D])
        X1 = at("X1", 4, [P, B, D])
        XTh = at("XTh", 8, [D, NTOK], F32R)
        XTl = at("XTl", 12, [D, NTOK], F32R)
        CV = at("CV", 16, [P, B, D])
        QP = at("QP", 20, [P, H, NTOK], BF16)
        KP = at("KP", 52, [P, H, NTOK], BF16)
        Mh = at("Mh", 84, [D, H, D], F32R)
        Ml = at("Ml", 92, [D, H, D], F32R)
        Vh = at("Vh", 100, [D, H, D], F32R)
        Vl = at("Vl", 108, [D, H, D], F32R)
        Th = at("Th", 116, [D, 2, GB, H, P], F32R)
        Tl = at("Tl", 148, [D, 2, GB, H, P], F32R)
        VP = at("VP", 180, [P, 3, HU * D])
        EX = at("EX", 186, [P, 3, HU * P])
        PTs = at("PTs", 192, [P, 3, HU * P])
        WK = at("WK", 132, [P, H * DH])
        WQ = at("WQ", 136, [P, H * DH])
        WV = at("WV", 140, [P, H * DH])
        WKT = at("WKT", 144, [P, 8, D])
        WVT = at("WVT", 164, [P, 8, D])
        WQBD = at("WQBD", 168, [P, 8, 2, D])
        WOBD = at("WOBD", 186, [P, 8, 2, D])
        XHAT = at("XHAT", 20, [P, B, D])
        XTF = at("XTF", 24, [D, NTOK])
        put = shelf(52, 84)
        CK = put("CK", [P, B, D])
        CKT = put("CKT", [P, B, D])
        KR = put("KR", [D, P])
        KT = put("KT", [D, 2, PARTS, P], BF16)
        BROW = put("BROW", [1, P])
        BRES = put("BRES", [1, P])
        BPT = put("BPT", [1, PARTS, P], BF16)
        SLI = put("SLI", [B, 1], I32)
        SLF = put("SLF", [B, 1])
        KIX = put("KIX", [B, P])
        MPT = put("MPT", [B, PARTS, P], BF16)
        put = shelf(116, 132)
        XV = put("XV", [P, B, H, VC], BF16)
        E32 = put("E32", [P, 2, HU * P])
        PXS = put("PXS", [P, 2, H, VC])
        NMX2 = put("NMX2", [P, 2, H])
        MXT = put("MXT", [H, 2, PARTS, P], BF16)
        MR = put("MR", [H, P])
        WTE = put("WTE", [P, GB, E])
        EH = at("EH", 172, [P, 4, HU * P], F16)
        EL = at("EL", 176, [P, 4, HU * P], F16)
        WH = [at("WGh", 148, [D, E, FI], F32R), at("WUh", 132, [D, E, FI], F32R)]
        WL = [at("WGl", 156, [D, E, FI], F32R), at("WUl", 140, [D, E, FI], F32R)]
        WD = at("WD", 164, [P, E, 2, D])
        GRAW = at("GRAW", 84, [P, 2 * E, D])
        URAW = at("URAW", 92, [P, 2 * E, D])
        DRAW = at("DRAW", 100, [P, E, 2, P])
        X2Th = at("X2Th", 84, [D, NG, GB * P], F32R)
        X2Tl = at("X2Tl", 88, [D, NG, GB * P], F32R)
        SG = at("SG", 92, [P, 2, 2, GB * P])
        HT = at("HT", 96, [P, 2, 2, GB * P])
        Z = at("Z", 100, [P, B, D])
        OUT = at("OUT", 104, [P, B, D])
        put = shelf(108, 116)
        LG, PR, EQ, HOT1, HOT2, WT = (put(n, [P, NG, GB, E]) for n in ("LG", "PR", "EQ", "HOT1", "HOT2", "WT"))
        ROWS = put("ROWS", [P, 8, GB])
        NUM = put("NUM", [P, D])
        XR = put("XR", [P, H])
        put = shelf(198, 207)
        ID = put("ID", [P, P])
        ONES = put("ONES", [P, P], BF16)
        Y = put("Y", [P, 2, D])
        QT = put("QT", [P, 2, PARTS, P], BF16)
        QR = put("QR", [D, P])
        QTN = put("QTN", [P, D])
        GBC = put("GBC", [P, 2])
        HALF = put("HALF", [P, B])
        NMX = put("NMX", [P, 4, HU])
        SUM = put("SUM", [P, 4, HU])
        RCP = put("RCP", [P, 4, HU])
        BST = put("BST", [P, B, 6])
        BMV = put("BMV", [P, B, 2])
        VE = put("VE", [P, B])
        RS = put("RS", [P, B])
        TST = put("TST", [P, 6])
        TMV = put("TMV", [P, 2, 2])
        TVE = put("TVE", [P, 2])
        TRS = put("TRS", [P, 2])
        RW = put("RW", [D, E])
        RWh = put("RWh", [D, E], F32R)
        RWl = put("RWl", [D, E], F32R)

        bank = [stack.enter_context(nc.psum_tensor(f"bank{i}", [P, 512], F32)) for i in range(8)]
        T_BANK, V_BANK, S_BANK, PT_BANK, ACC = 0, 1, (2, 3), 4, 6
        G_BANK, U_BANK, ST_BANK, PX_BANK, SX_BANK, Y_BANK = 0, 1, (2, 3), 4, 5, 6
        TURNED = bank[7][:, 0:P]
        MX_T = bank[7][0:H, P:2 * P]
        ROUTER = bank[7][:, 2 * P:2 * P + GB * E]

        dram = lambda name, shape, dt: nc.dram_tensor(name, shape, dt, kind="Internal").ap()
        k_rows = dram("k_rows", [PARTS, PARTS, XH * H, NTOK], BF16)
        q_rows = dram("q_rows", [B, PARTS, PARTS, XH * H, P], BF16)
        m_rows = dram("m_rows", [B, PARTS * H, P], BF16)
        bias_rows = dram("bias_rows", [PARTS, P], BF16)
        mask_rows = dram("mask_rows", [B, PARTS, P], BF16)

        names = """x_in wk_in wq_in wv_in wo_in gb_in ck_in cv_in rw_in rows_in gate_in up_in down_in
            ident zeroed ones_ready consts stats_x rstd_x xhat_done dve_link pool_link setup_full xtf_done
            xth_done xtl_done mh_done oh_done t_full th_done tl_done s_full max_done exp_done sum_recip
            p_norm v_full v_done px_read sums_added pt_full pt_done pv_full y_added var_ready rstd_ready x_normed
            kt_full kh_done kr_done kt_done qh_done ck_turned k_rows_in rows_ready rows_out kp_in one_rows qt_full qt_done
            sx_full maxx_done mt_full mxh_done mxr_done mt_done st_full eh_done e32_done el_done px_full
            num_done x2_normed x2t_full x2h_done x2l_done rw_split router_full router_read
            route_exp weights_ready vparts_ready w_full wh_done w_done g_full u_full tanh_done gated hu_done
            dn_full y_acc last_var last_rstd out_ready stored""".split()
        s = {n: sem(n) for n in names}
        set_done = [sem(f"setup_done{i}") for i in range(16)]
        q_out = [sem(f"q_out{b}") for b in range(B)]
        q_in = [sem(f"q_in{b}") for b in range(B)]
        m_out = [sem(f"m_out{b}") for b in range(B)]
        m_in = [sem(f"m_in{b}") for b in range(B)]
        k_out = [sem(f"k_out{i}") for i in range(2)]
        block = stack.enter_context(nc.Block())

        K0, Q0, X0, M0, WV0, O0 = 0, 2, 4, 6, 10, 12
        sbank = lambda i: bank[2 + i % 4]
        unit = lambda n: (n // UB, n % UB)

        def due(n, first, every, count):
            i, off = divmod(n - first, every)
            return i if off == 0 and 0 <= i < count else None

        k_step = lambda b: 2 * b + 3
        q_step = lambda b: UB * b + TAIL + 2

        @block.sync
        def _(sp):
            sp.dma_start(X[:, :, :], x_in.rearrange("b s d -> s b d")).then_inc(s["x_in"], 16)
            sp.dma_start(WQ[:, :], wq).then_inc(s["wq_in"], 16)
            sp.dma_start(WV[:, :], wv).then_inc(s["wv_in"], 16)
            sp.wait_ge(s["zeroed"], 2)
            for j in range(2):
                sp.dma_start(WOBD[DH * j:DH * j + DH, :, j, :],
                             wo.rearrange("(c j p) n -> j p c n", j=2, p=DH)[j]).then_inc(s["wo_in"], 16)
            sp.dma_start(CK[:, :, :], ctx_in[:, :, 0:D].rearrange("b s d -> s b d")).then_inc(s["ck_in"], 16)
            sp.dma_start(BROW[:, :], key_bias.rearrange("(a k) -> a k", a=1)).then_inc(s["rows_in"], 16)
            sp.dma_start(SLI[:, :], seq_len).then_inc(s["rows_in"], 16)
            sp.dma_start(CV[:, :, :], ctx_in[:, :, D:2 * D].rearrange("b s d -> s b d")).then_inc(s["cv_in"], 16)
            sp.wait_ge(s["rows_ready"], 1)
            sp.dma_start(bias_rows.rearrange("(a p) k -> a p k", a=1), BPT[:, :, :]).then_inc(s["rows_out"], 16)
            sp.dma_start(mask_rows, MPT[:, :, :]).then_inc(s["rows_out"], 16)

            def keys_out(b):
                sp.wait_ge(s["kt_done"], b + 1)
                for i in range(PARTS):
                    sp.dma_start(k_rows[i].rearrange("j r k -> r j k")[:, :, b * P:(b + 1) * P],
                                 KT[:, b % 2, :, :]).then_inc(k_out[b % 2], 16)

            def queries(b):
                sp.wait_ge(s["qt_done"], b + 1)
                for j in range(PARTS):
                    sp.dma_start(q_rows[b].rearrange("i j r q -> j r i q")[j], QT[:, b % 2, :, :]).then_inc(q_out[b], 16)
                sp.wait_ge(q_out[b], 16 * PARTS)
                sp.dma_start(QP[0:KROWS, :, b * P:(b + 1) * P],
                             q_rows[b].rearrange("i j (d h) q -> (i j d) h q", h=H)).then_inc(q_in[b], 16)

            def keys_in():
                for i in range(2):
                    sp.wait_ge(k_out[i], 16 * PARTS * B // 2)
                sp.wait_ge(s["rows_out"], 32)
                sp.dma_start(KP[0:KROWS, :, :],
                             k_rows.rearrange("i j (d h) k -> (i j d) h k", h=H)).then_inc(s["kp_in"], 16)
                sp.dma_start(KP[KROWS:KROWS + PARTS, :, :].rearrange("r h (b k) -> r (h b) k", k=P),
                             bias_rows[:, None, :].broadcast_to([PARTS, H * B, P])).then_inc(s["kp_in"], 16)
                for b in range(B):
                    sp.dma_start(KP[KROWS + PARTS:KMAX, :, b * P:(b + 1) * P],
                                 mask_rows[b, :, None, :].broadcast_to([PARTS, H, P])).then_inc(s["kp_in"], 16)
                sp.dma_start(KP[KMAX:KALL, :, :].rearrange("r h (b k) -> r (h b) k", k=P),
                             ONES[0:PARTS, None, :].broadcast_to([PARTS, H * B, P])).then_inc(s["kp_in"], 16)

            sp.wait_ge(s["ones_ready"], 1)
            sp.wait_ge(s["xtl_done"], 2)
            sp.dma_start(QP[KROWS:KMAX, :, :].rearrange("r h (b q) -> r (h b) q", q=P),
                         ONES[0:KMAX - KROWS, None, :].broadcast_to([KMAX - KROWS, H * B, P])).then_inc(s["one_rows"], 16)
            for n in range(STEPS):
                if (b := due(n, k_step(0), 2, B)) is not None:
                    keys_out(b)
                    if b == B - 1:
                        keys_in()
                if (b := due(n, q_step(0), UB, B)) is not None:
                    queries(b)
                if n == TG * (NG - 1):
                    sp.wait_ge(s["t_full"], NT)
                    sp.dma_start(GRAW[:, :, :], gate_w.rearrange("e (c p) h -> p (e c) h", p=P)).then_inc(s["gate_in"], 16)
                    sp.dma_start(URAW[:, :, :], up_w.rearrange("e (c p) h -> p (e c) h", p=P)).then_inc(s["up_in"], 16)
                if n == NU + 2:
                    sp.wait_ge(s["v_full"], NU)
                    sp.dma_start(DRAW[:, :, :, :], down_w.rearrange("e h (c i) -> h e c i", c=2)).then_inc(s["down_in"], 16)
                for x in x_items(n):
                    if (b := due(x, UB, UB, B)) is not None:
                        sp.wait_ge(s["mt_done"], b + 1)
                        sp.dma_start(m_rows[b].rearrange("(p h) q -> h p q", h=H), MXT[:, b % 2, :, :]).then_inc(m_out[b], 16)
                        sp.wait_ge(m_out[b], 16)
                        sp.dma_start(QP[KMAX:KALL, :, b * P:(b + 1) * P],
                                     m_rows[b].rearrange("(p h) q -> p h q", h=H)).then_inc(m_in[b], 16)
                if (grp := due(n, F0 + E + 1, E, NG)) is not None:
                    for b in range(GB * grp, GB * grp + GB):
                        sp.wait_ge(s["out_ready"], b + 1)
                        sp.dma_start(out[b], OUT[:, b, :]).then_inc(s["stored"], 16)
            sp.wait_ge(s["stored"], 16 * B)

        @block.gpsimd
        def _(pool):
            g = nc.gpsimd
            chain = [0]

            def link(ins):
                chain[0] += 1
                ins.then_inc(s["pool_link"], 1)
                pool.wait_ge(s["pool_link"], chain[0])

            link(g.memset(ID[:, :], 0.0))
            g.affine_select(out=ID[:, :], in_=ID[:, :], compare_op=ALU.not_equal, fill=1.0, base=0,
                            pattern=[[-1, P]], channel_multiplier=1).then_inc(s["ident"], 1)
            link(g.memset(HALF[:, :], -0.5))
            g.memset(WQBD[:, :, :, :], 0.0).then_inc(s["zeroed"], 1)
            g.memset(WOBD[:, :, :, :], 0.0).then_inc(s["zeroed"], 1)
            g.memset(ONES[:, :], 1.0).then_inc(s["ones_ready"], 1)
            pool.wait_ge(s["stats_x"], 1)
            g.tensor_tensor(RS[:, :], VE[:, :], HALF[:, :], ALU.pow).then_inc(s["rstd_x"], 1)
            pool.wait_ge(s["rows_in"], 32)
            link(g.iota(KIX[:, :], pattern=[[1, P]], base=0, channel_multiplier=0,
                        allow_small_or_imprecise_dtypes=True))
            link(g.tensor_copy(SLF[:, :], SLI[:, :]))
            for p, c in enumerate(mask_parts()):
                link(g.tensor_scalar(MPT[:, p, :], KIX[:, :], SLF[:, 0:1], c, ALU.is_ge, ALU.mult))
            link(g.tensor_copy(BPT[:, 0, :], BROW[:, :]))
            link(g.tensor_tensor(BRES[:, :], BROW[:, :], BPT[:, 0, :], ALU.subtract))
            link(g.tensor_copy(BPT[:, 1, :], BRES[:, :]))
            link(g.tensor_tensor(BRES[:, :], BRES[:, :], BPT[:, 1, :], ALU.subtract))
            g.tensor_copy(BPT[:, 2, :], BRES[:, :]).then_inc(s["rows_ready"], 1)
            pool.wait_ge(s["rows_ready"], 1)

            def deviation(i):
                pool.wait_ge(s["var_ready"], i + 1)
                g.tensor_tensor(TRS[:, i % 2:i % 2 + 1], TVE[:, i % 2:i % 2 + 1], HALF[:, 0:1],
                                ALU.pow).then_inc(s["rstd_ready"], 1)

            for n in range(STEPS):
                if (b := due(n, TAIL, UB, B)) is not None:
                    deviation(b)
                if n < NU:
                    pool.wait_ge(s["sum_recip"], n + 1)
                    e = EX[:, n % 3, :].rearrange("q (h k) -> q h k", h=HU)
                    g.tensor_tensor(e, e, RCP[:, n % 4, :, None].broadcast_to([P, HU, P]), ALU.mult).then_inc(s["p_norm"], 1)
                if (b := due(n, k_step(0), 2, B)) is not None:
                    pool.wait_ge(s["kr_done"], b + 1)
                    link(g.tensor_copy(KT[:, b % 2, 1, :], KR[:, :]))
                    g.tensor_tensor(KT[:, b % 2, 2, :], KR[:, :], KT[:, b % 2, 1, :], ALU.subtract).then_inc(s["kt_done"], 1)
                if (b := due(n, XS + 1, 2, B)) is not None:
                    if b == 0:
                        pool.wait_ge(s["cv_in"], 16)
                        pool.wait_ge(s["s_full"], TG * (NG - 1))
                        link(g.memset(XV[:, :, :, :].rearrange("k b h c -> k (b h c)"), 1.0))
                        g.iota(WTE[:, :, :], pattern=[[0, GB], [-1, E]], base=E, channel_multiplier=0,
                               allow_small_or_imprecise_dtypes=True).then_inc(s["consts"], 1)
                    src = CV[:, b, :].rearrange("k (h d) -> k h d", h=H)
                    part = lambda p: XV[:, b, :, p * XH:(p + 1) * XH]
                    link(g.tensor_copy(part(0), src))
                    link(g.tensor_tensor(src, src, part(0), ALU.subtract))
                    link(g.tensor_copy(part(1), src))
                    g.tensor_tensor(part(2), src, part(1), ALU.subtract).then_inc(s["vparts_ready"], 1)
                for x in x_items(n):
                    if (b := due(x, UB, UB, B)) is not None:
                        pool.wait_ge(s["mxr_done"], b + 1)
                        link(g.tensor_copy(MXT[:, b % 2, 1, :], MR[:, :]))
                        g.tensor_tensor(MXT[:, b % 2, 2, :], MR[:, :], MXT[:, b % 2, 1, :], ALU.subtract).then_inc(s["mt_done"], 1)
                    m = x - ST_LAG
                    if 0 <= m < NU:
                        pool.wait_ge(s["e32_done"], m + 1)
                        if m >= 4:
                            pool.wait_ge(s["px_full"], m - 3)
                        g.tensor_tensor(EL[:, m % 4, :], E32[:, m % 2, :], EH[:, m % 4, :], ALU.subtract).then_inc(s["el_done"], 1)
                    if (b := due(x, XTAIL, UB, B)) is not None:
                        pool.wait_ge(s["px_read"], b + 1)
                        part = lambda p: PXS[:, b % 2, :, p * XH:(p + 1) * XH]
                        num = NUM[:, :].rearrange("q (h d) -> q h d", h=H)
                        if b:
                            pool.wait_ge(s["sums_added"], b)
                        link(g.tensor_tensor(num, part(1), part(2), ALU.add))
                        link(g.tensor_tensor(num, num, part(0), ALU.add))
                    if (b := due(x, XTAIL + 1, UB, B)) is not None:
                        num = NUM[:, :].rearrange("q (h d) -> q h d", h=H)
                        pool.wait_ge(s["num_done"], b + 1)
                        link(g.tensor_tensor(num, num, XR[:, :, None].broadcast_to([P, H, XH]), ALU.mult))
                        pool.wait_ge(s["x_normed"], B)
                        if b >= 2:
                            pool.wait_ge(s["x2_normed"], b - 1)
                        g.tensor_tensor(Y[:, b % 2, :], NUM[:, :], X1[:, b, :], ALU.add).then_inc(s["sums_added"], 1)
                    if (b := due(x, XTAIL + 2, UB, B)) is not None:
                        deviation(B + b)
                if (grp := due(n, F0 + E + 1, E, NG)) is not None:
                    pool.wait_ge(s["last_var"], grp + 1)
                    gb = slice(GB * grp, GB * grp + GB)
                    g.tensor_tensor(RS[:, gb], VE[:, gb], HALF[:, gb], ALU.pow).then_inc(s["last_rstd"], 1)

        @block.scalar
        def _(act):
            a = nc.scalar
            act.dma_start(WK[:, :], wk).then_inc(s["wk_in"], 16)
            act.dma_start(GBC[:, 0:1], gamma.rearrange("(d a) -> d a", a=1)).then_inc(s["gb_in"], 16)
            act.dma_start(GBC[:, 1:2], beta.rearrange("(d a) -> d a", a=1)).then_inc(s["gb_in"], 16)
            act.dma_start(RW[:, :], router_w.rearrange("e h -> h e"), allow_slow_non_contiguous=True).then_inc(s["rw_in"], 16)

            def setup(i, out_ap, then):
                act.wait_ge(s["setup_full"], i + 1)
                a.activation(out_ap, sbank(i)[:, :], ACT.Copy).then_inc(then, 1)

            def t_high(t):
                grp, pair = divmod(t, TG)
                act.wait_ge(s["t_full"], t + 1)
                b_ = bank[t % 2] if t < TG else bank[T_BANK]
                a.activation(Th[:, grp % 2, :, 2 * pair:2 * pair + 2, :].rearrange("d b h k -> d h b k"),
                             b_[:, :].rearrange("d (h b k) -> d h b k", h=2, b=GB), ACT.Copy).then_inc(s["th_done"], 1)

            for i in range(2):
                setup(K0 + i, WKT[:, 4 * i:4 * i + 4, :], set_done[K0 + i])
            for i in range(2):
                act.wait_ge(s["xtf_done"], i + 1)
                a.activation(XTh[:, 512 * i:512 * i + 512], XTF[:, 512 * i:512 * i + 512], ACT.Copy).then_inc(s["xth_done"], 1)
            for i in range(4):
                setup(M0 + i, Mh[:, 4 * i:4 * i + 4, :], s["mh_done"])
            for i in range(2):
                setup(WV0 + i, WVT[:, 4 * i:4 * i + 4, :], set_done[WV0 + i])
            for i in range(4):
                t_high(2 * i)
                t_high(2 * i + 1)
                setup(O0 + i, Vh[:, 4 * i:4 * i + 4, :], s["oh_done"])
            for n in range(STEPS):
                k = n - PV_LAG
                if 0 <= k < NU:
                    act.wait_ge(s["v_full"], k + 1)
                    if k >= 3:
                        act.wait_ge(s["pv_full"], k - 2)
                    a.activation(VP[:, k % 3, :], bank[V_BANK][:, :], ACT.Copy).then_inc(s["v_done"], 1)
                if n + TG < NT:
                    t_high(n + TG)
                if n < NU:
                    act.wait_ge(s["max_done"], n + 1)
                    if n >= 3:
                        act.wait_ge(s["pt_full"], n - 2)
                    for j in range(HU):
                        ins = a.activation(EX[:, n % 3, j * P:(j + 1) * P], bank[S_BANK[n % 2]][:, j * P:(j + 1) * P],
                                           ACT.Exp, bias=NMX[:, n % 4, j:j + 1], accum_out=SUM[:, n % 4, j:j + 1])
                    ins.then_inc(s["exp_done"], 1)
                if (b := due(n, k_step(0), 2, B)) is not None:
                    act.wait_ge(s["kt_full"], b + 1)
                    if b >= 2:
                        act.wait_ge(k_out[b % 2], 16 * PARTS * (b // 2))
                    a.activation(KT[:, b % 2, 0, :], TURNED, ACT.Copy).then_inc(s["kh_done"], 1)
                if (b := due(n, q_step(0), UB, B)) is not None:
                    act.wait_ge(s["qt_full"], b + 1)
                    if b >= 2:
                        act.wait_ge(q_out[b - 2], 16 * PARTS)
                    a.activation(QT[:, b % 2, 0, :], TURNED, ACT.Copy, scale=float(XH) ** -0.5).then_inc(s["qh_done"], 1)
                if (w := due(n, W0, 1, 3 * UB)) is not None:
                    act.wait_ge(s["w_full"], w + 1)
                    es = slice(2 * (w % 4), 2 * (w % 4) + 2)
                    if w < 8:
                        a.activation(WH[w // 4][:, es, :], bank[T_BANK][:, :].rearrange("h (e i) -> h e i", e=2),
                                     ACT.Copy).then_inc(s["wh_done"], 1)
                    else:
                        a.activation(WD[:, es, :, :], bank[T_BANK][:, :].rearrange("i (e c h) -> i e c h", e=2, c=2),
                                     ACT.Copy, scale=0.5).then_inc(s["w_done"], 1)
                f = n - F0
                if 0 <= f < NF:
                    act.wait_ge(s["g_full"], f + 1)
                    if f >= 2:
                        act.wait_ge(s["hu_done"], f - 1)
                    a.activation(SG[:, f % 2, :, :].rearrange("i c t -> i (c t)"), bank[G_BANK][:, :],
                                 ACT.Tanh, scale=0.5).then_inc(s["tanh_done"], 1)
                for x in x_items(n):
                    if (b := due(x, UB, UB, B)) is not None:
                        act.wait_ge(s["mt_full"], b + 1)
                        if b >= 2:
                            act.wait_ge(m_out[b - 2], 16)
                        a.activation(MXT[:, b % 2, 0, :], MX_T, ACT.Copy).then_inc(s["mxh_done"], 1)
                    if (b := due(x, XTAIL, UB, B)) is not None:
                        act.wait_ge(s["px_full"], UB * b + UB)
                        if b >= 2:
                            act.wait_ge(s["sums_added"], b - 1)
                            act.wait_ge(s["num_done"], b - 1)
                        a.activation(PXS[:, b % 2, :, :].rearrange("q h c -> q (h c)"), bank[PX_BANK][:, 0:H * VC],
                                     ACT.Copy).then_inc(s["px_read"], 1)
                    m = x - ST_LAG
                    if 0 <= m < NU:
                        act.wait_ge(s["st_full"], m + 1)
                        if m >= 4:
                            act.wait_ge(s["px_full"], m - 3)
                        if m >= 2:
                            act.wait_ge(s["el_done"], m - 1)
                        if m == 0:
                            act.wait_ge(s["s_full"], NU)
                        a.activation(EH[:, m % 4, :], bank[ST_BANK[m % 2]][:, :], ACT.Exp).then_inc(s["eh_done"], 1)
                        a.activation(E32[:, m % 2, :], bank[ST_BANK[m % 2]][:, :], ACT.Exp).then_inc(s["e32_done"], 1)
                    if (b := due(x, X2T, UB, B)) is not None:
                        act.wait_ge(s["x2t_full"], b + 1)
                        grp, half = divmod(b, GB)
                        if b == 0:
                            act.wait_ge(s["w_full"], UB)
                        a.activation(X2Th[:, grp, half * P:(half + 1) * P], TURNED, ACT.Copy).then_inc(s["x2h_done"], 1)
                    if (grp := due(x, UB * (GB - 1) + ROUTE, UB * GB, NG)) is not None:
                        act.wait_ge(s["router_read"], grp + 1)
                        a.activation(PR[:, grp, :, :], LG[:, grp, :, :], ACT.Exp).then_inc(s["route_exp"], 1)

        @block.vector
        def _(dve):
            v = nc.vector
            chain = [0]

            def mark(ins):
                chain[0] += 1
                ins.then_inc(s["dve_link"], 1)

            def link(ins):
                mark(ins)
                dve.wait_ge(s["dve_link"], chain[0])

            dve.wait_ge(s["x_in"], 16)
            for b in range(B):
                ins = v.bn_stats(BST[:, b, :], X[:, b, :])
            link(ins)
            for b in range(B):
                ins = v.bn_aggr(BMV[:, b, :], BST[:, b, :])
            link(ins)
            v.tensor_scalar(VE[:, :], BMV[:, :, 1], EPS, None, ALU.add).then_inc(s["stats_x"], 1)
            dve.wait_ge(s["zeroed"], 1)
            for i in range(2):
                dve.wait_ge(s["setup_full"], Q0 + i + 1)
                for j in range(2):
                    ins = v.tensor_scalar(WQBD[DH * j:DH * j + DH, 4 * i:4 * i + 4, j, :],
                                          sbank(Q0 + i)[DH * j:DH * j + DH, :].rearrange("p (c d) -> p c d", c=4),
                                          float(DH) ** -0.5, None, ALU.mult)
                ins.then_inc(set_done[Q0 + i], 1)
            dve.wait_ge(s["rstd_x"], 1)
            for b in range(B):
                v.tensor_scalar(XHAT[:, b, :], X[:, b, :], BMV[:, b, 0:1], RS[:, b:b + 1], ALU.subtract,
                                ALU.mult).then_inc(s["xhat_done"], 1)
            dve.wait_ge(s["gb_in"], 32)
            for i in range(2):
                c = slice(512 * i, 512 * i + 512)
                dve.wait_ge(s["setup_full"], X0 + i + 1)
                v.tensor_scalar(XTF[:, c], sbank(X0 + i)[:, :], GBC[:, 0:1], GBC[:, 1:2], ALU.mult,
                                ALU.add).then_inc(s["xtf_done"], 1)
            for i in range(2):
                c = slice(512 * i, 512 * i + 512)
                dve.wait_ge(s["xth_done"], i + 1)
                v.tensor_tensor(XTl[:, c], XTF[:, c], XTh[:, c].bitcast(F32), ALU.subtract).then_inc(s["xtl_done"], 1)

            def low_weights(i, item, high, low_):
                hs = slice(4 * i, 4 * i + 4)
                v.tensor_tensor(low_[:, hs, :], sbank(item)[:, :].rearrange("p (h d) -> p h d", h=4),
                                high[:, hs, :].bitcast(F32), ALU.subtract).then_inc(set_done[item], 1)

            def t_low(t):
                grp, pair = divmod(t, TG)
                dve.wait_ge(s["th_done"], t + 1)
                b_ = bank[t % 2] if t < TG else bank[T_BANK]
                to = lambda T: T[:, grp % 2, :, 2 * pair:2 * pair + 2, :].rearrange("d b h k -> d h b k")
                v.tensor_tensor(to(Tl), b_[:, :].rearrange("d (h b k) -> d h b k", h=2, b=GB), to(Th).bitcast(F32),
                                ALU.subtract).then_inc(s["tl_done"], 1)

            for i in range(4):
                dve.wait_ge(s["mh_done"], i + 1)
                low_weights(i, M0 + i, Mh, Ml)
            for i in range(4):
                t_low(2 * i)
                t_low(2 * i + 1)
                dve.wait_ge(s["oh_done"], i + 1)
                low_weights(i, O0 + i, Vh, Vl)
            dve.wait_ge(s["rw_in"], 16)
            v.tensor_copy(RWh[:, :], RW[:, :]).then_inc(s["rw_split"], 1)
            dve.wait_ge(s["rw_split"], 1)
            v.tensor_tensor(RWl[:, :], RW[:, :], RWh[:, :].bitcast(F32), ALU.subtract).then_inc(s["rw_split"], 1)

            dve.wait_ge(s["ck_in"], 16)
            v.tensor_copy(CKT[:, :, :].rearrange("k b (d h) -> k b h d", h=H),
                          CK[:, :, :].rearrange("k b (h d) -> k b h d", h=H)).then_inc(s["ck_turned"], 1)

            def statistics(i, y):
                link(v.bn_stats(TST[:, :], y))
                link(v.bn_aggr(TMV[:, i % 2, :], TST[:, :]))
                v.tensor_scalar(TVE[:, i % 2:i % 2 + 1], TMV[:, i % 2, 1:2], EPS, None, ALU.add).then_inc(s["var_ready"], 1)

            def normalise(i, to, y):
                dve.wait_ge(s["rstd_ready"], i + 1)
                return v.tensor_scalar(to, y, TMV[:, i % 2, 0:1], TRS[:, i % 2:i % 2 + 1], ALU.subtract, ALU.mult)

            def route(grp, part):
                q = grp
                row = lambda i: ROWS[:, i, :]
                wide = lambda i: ROWS[:, i, :, None].broadcast_to([P, GB, E])
                pr, eq, lg = PR[:, q, :, :], EQ[:, q, :, :], LG[:, q, :, :]
                hots = HOT1[:, q, :, :], HOT2[:, q, :, :]
                dve.wait_ge(s["dve_link"], chain[0])
                if part == 0:
                    dve.wait_ge(s["router_full"], GB * (grp + 1))
                    router = ROUTER.rearrange("t (b e) -> t b e", b=GB)
                    link(v.tensor_reduce(row(0), router, axis=AX_X, op=ALU.max))
                    v.tensor_tensor(lg, router, wide(0), ALU.subtract).then_inc(s["router_read"], 1)
                elif part == 1:
                    dve.wait_ge(s["route_exp"], grp + 1)
                    link(v.tensor_reduce(row(1), pr, axis=AX_X, op=ALU.add))
                    link(v.reciprocal(row(2), row(1)))
                    mark(v.tensor_tensor(pr, pr, wide(2), ALU.mult))
                elif part in (2, 3):
                    k = part - 2
                    src = lg if k else pr
                    dve.wait_ge(s["consts"], 1)
                    link(v.tensor_reduce(row(3 + k), src, axis=AX_X, op=ALU.max))
                    link(v.tensor_tensor(eq, src, wide(3 + k), ALU.is_equal))
                    link(v.tensor_tensor(eq, eq, WTE[:, :, :], ALU.mult))
                    link(v.tensor_reduce(row(5), eq, axis=AX_X, op=ALU.max))
                    if k == 0:
                        link(v.tensor_tensor(hots[0], eq, wide(5), ALU.is_equal))
                        mark(v.scalar_tensor_tensor(lg, hots[0], -2.0, pr, ALU.mult, ALU.add))
                    else:
                        mark(v.tensor_tensor(hots[1], eq, wide(5), ALU.is_equal))
                else:
                    mark(v.tensor_tensor(row(6), row(3), row(4), ALU.add))
                    link(v.tensor_tensor(eq, hots[0], hots[1], ALU.add))
                    mark(v.reciprocal(row(7), row(6)))
                    link(v.tensor_tensor(eq, eq, pr, ALU.mult))
                    v.tensor_tensor(WT[:, q, :, :], eq, wide(7), ALU.mult).then_inc(s["weights_ready"], 1)

            def scores_max(x):
                b, u = unit(x)
                if u == 0 and b >= 2:
                    dve.wait_ge(s["mt_full"], b - 1)
                dve.wait_ge(s["sx_full"], x + 1)
                v.tensor_reduce(NMX2[:, b % 2, HU * u:HU * u + HU],
                                bank[SX_BANK][:, :].rearrange("q (h k) -> q h k", h=HU),
                                axis=AX_X, op=ALU.max, negate=True).then_inc(s["maxx_done"], 1)

            def x_item(x):
                if 0 <= x < NU:
                    scores_max(x)
                if (b := due(x, UB, UB, B)) is not None:
                    dve.wait_ge(s["mxh_done"], b + 1)
                    if b:
                        dve.wait_ge(s["mt_done"], b)
                    v.tensor_tensor(MR[:, :], MX_T, MXT[:, b % 2, 0, :], ALU.subtract).then_inc(s["mxr_done"], 1)
                if (b := due(x, XTAIL + 1, UB, B)) is not None:
                    dve.wait_ge(s["px_read"], b + 1)
                    if b:
                        dve.wait_ge(s["sums_added"], b)
                    v.reciprocal(XR[:, :], PXS[:, b % 2, :, VC - 1]).then_inc(s["num_done"], 1)
                if (b := due(x, XTAIL + 2, UB, B)) is not None:
                    dve.wait_ge(s["sums_added"], b + 1)
                    statistics(B + b, Y[:, b % 2, :])
                if (b := due(x, XTAIL + 3, UB, B)) is not None:
                    normalise(B + b, X2[:, b, :], Y[:, b % 2, :]).then_inc(s["x2_normed"], 1)
                if (b := due(x, X2T + 1, UB, B)) is not None:
                    grp, half = divmod(b, GB)
                    dve.wait_ge(s["x2h_done"], b + 1)
                    c = slice(half * P, (half + 1) * P)
                    v.tensor_tensor(X2Tl[:, grp, c], TURNED, X2Th[:, grp, c].bitcast(F32),
                                    ALU.subtract).then_inc(s["x2l_done"], 1)
                for part in range(5):
                    if (grp := due(x, UB * (GB - 1) + ROUTE + part, UB * GB, NG)) is not None:
                        route(grp, part)

            for n in range(STEPS):
                if n < NU:
                    dve.wait_ge(s["s_full"], n + 1)
                    v.tensor_reduce(NMX[:, n % 4, :], bank[S_BANK[n % 2]][:, :].rearrange("q (h k) -> q h k", h=HU),
                                    axis=AX_X, op=ALU.max, negate=True).then_inc(s["max_done"], 1)
                if n + TG < NT:
                    t_low(n + TG)
                k = n - PT_LAG
                if 0 <= k < NU:
                    dve.wait_ge(s["pt_full"], k + 1)
                    if k >= 3:
                        dve.wait_ge(s["pv_full"], k - 2)
                    v.tensor_copy(PTs[:, k % 3, :], bank[PT_BANK][:, :]).then_inc(s["pt_done"], 1)
                if (b := due(n, TAIL + 1, UB, B)) is not None:
                    normalise(b, X1[:, b, :], Y[:, b % 2, :])
                    if b:
                        dve.wait_ge(s["qt_full"], b)
                    normalise(b, QTN[:, :].rearrange("t (d h) -> t h d", h=H),
                              Y[:, b % 2, :].rearrange("t (h d) -> t h d", h=H)).then_inc(s["x_normed"], 1)
                if (b := due(n, TAIL, UB, B)) is not None:
                    dve.wait_ge(s["pv_full"], UB * b + UB)
                    v.tensor_tensor(Y[:, b % 2, :], bank[ACC][:, 0:D], X[:, b, :], ALU.add).then_inc(s["y_added"], 1)
                    dve.wait_ge(s["y_added"], b + 1)
                    statistics(b, Y[:, b % 2, :])
                if (b := due(n, q_step(0), UB, B)) is not None:
                    dve.wait_ge(s["qh_done"], b + 1)
                    link(v.scalar_tensor_tensor(QR[:, :], TURNED, float(XH) ** -0.5, QT[:, b % 2, 0, :], ALU.mult,
                                                ALU.subtract))
                    link(v.tensor_copy(QT[:, b % 2, 1, :], QR[:, :]))
                    v.tensor_tensor(QT[:, b % 2, 2, :], QR[:, :], QT[:, b % 2, 1, :], ALU.subtract).then_inc(s["qt_done"], 1)
                if (b := due(n, k_step(0), 2, B)) is not None:
                    dve.wait_ge(s["kh_done"], b + 1)
                    if b:
                        dve.wait_ge(s["kt_done"], b)
                    v.tensor_tensor(KR[:, :], TURNED, KT[:, b % 2, 0, :], ALU.subtract).then_inc(s["kr_done"], 1)
                if n < NU:
                    dve.wait_ge(s["exp_done"], n + 1)
                    v.reciprocal(RCP[:, n % 4, :], SUM[:, n % 4, :]).then_inc(s["sum_recip"], 1)
                if (w := due(n, W0, 1, 2 * UB)) is not None:
                    dve.wait_ge(s["wh_done"], w + 1)
                    es = slice(2 * (w % 4), 2 * (w % 4) + 2)
                    v.tensor_tensor(WL[w // 4][:, es, :], bank[T_BANK][:, :].rearrange("h (e i) -> h e i", e=2),
                                    WH[w // 4][:, es, :].bitcast(F32), ALU.subtract).then_inc(s["w_done"], 1)
                items = x_items(n)
                f = n - F0
                if 0 <= f < NF:
                    dve.wait_ge(s["tanh_done"], f + 1)
                    gated = SG[:, f % 2, :, :].rearrange("i c t -> i (c t)")
                    v.scalar_tensor_tensor(gated, gated, 1.0, bank[G_BANK][:, :], ALU.add, ALU.mult).then_inc(s["gated"], 1)
                if items:
                    x_item(items[0])
                if 0 <= f < NF:
                    dve.wait_ge(s["gated"], f + 1)
                    dve.wait_ge(s["u_full"], f + 1)
                    if f >= 2:
                        dve.wait_ge(s["dn_full"], f - 1)
                    v.tensor_tensor(HT[:, f % 2, :, :].rearrange("i c t -> i (c t)"), bank[U_BANK][:, :], gated,
                                    ALU.mult).then_inc(s["hu_done"], 1)
                if items[1:]:
                    x_item(items[1])
                f = n - F0 - 1
                if 0 <= f < NF:
                    grp, e = divmod(f, E)
                    dve.wait_ge(s["dn_full"], f + 1)
                    if e == 0:
                        dve.wait_ge(s["weights_ready"], grp + 1)
                    else:
                        dve.wait_ge(s["y_acc"], f)
                    for half in range(GB):
                        b = GB * grp + half
                        ins = v.scalar_tensor_tensor(Z[:, b, :], bank[Y_BANK][:, half * D:(half + 1) * D],
                                                     WT[:, grp, half, e:e + 1], (X2 if e == 0 else Z)[:, b, :],
                                                     ALU.mult, ALU.add)
                    ins.then_inc(s["y_acc"], 1)
                if (grp := due(n, F0 + E, E, NG)) is not None:
                    dve.wait_ge(s["y_acc"], E * (grp + 1))
                    bs = range(GB * grp, GB * grp + GB)
                    for b in bs:
                        ins = v.bn_stats(BST[:, b, :], Z[:, b, :])
                    link(ins)
                    for b in bs:
                        ins = v.bn_aggr(BMV[:, b, :], BST[:, b, :])
                    link(ins)
                    v.tensor_scalar(VE[:, bs[0]:bs[0] + GB], BMV[:, bs[0]:bs[0] + GB, 1], EPS, None,
                                    ALU.add).then_inc(s["last_var"], 1)
                if (grp := due(n, F0 + E + 1, E, NG)) is not None:
                    dve.wait_ge(s["last_rstd"], grp + 1)
                    for b in range(GB * grp, GB * grp + GB):
                        v.tensor_scalar(OUT[:, b, :], Z[:, b, :], BMV[:, b, 0:1], RS[:, b:b + 1], ALU.subtract,
                                        ALU.mult).then_inc(s["out_ready"], 1)

        @block.tensor
        def _(pe):
            mm = nc.tensor.matmul
            turn = nc.tensor.transpose

            def split_mm(out_ap, ah, al, bh, bl):
                mm(out_ap, ah, bh, start=True, stop=False)
                mm(out_ap, ah, bl, start=False, stop=False)
                return mm(out_ap, al, bh, start=False, stop=True)

            pe.wait_ge(s["ident"], 1)

            def room(i):
                if i >= 4:
                    j = i - 4
                    if X0 <= j < X0 + 2:
                        pe.wait_ge(s["xtf_done"], j - X0 + 1)
                    else:
                        pe.wait_ge(set_done[j], 1)

            def transposes(i, src):
                room(i)
                for j in range(4):
                    ins = turn(sbank(i)[:, j * P:(j + 1) * P], src(j), ID[:, :])
                ins.then_inc(s["setup_full"], 1)

            def weight_product(i0, i, wt, bd):
                room(i0 + i)
                for j in range(2):
                    c = 2 * i + j
                    ins = mm(sbank(i0 + i)[:, 2 * D * j:2 * D * (j + 1)], wt[:, c, :],
                             bd[:, c, :, :].rearrange("p j d -> p (j d)"), start=True, stop=True)
                ins.then_inc(s["setup_full"], 1)

            def t_product(t):
                grp, pair = divmod(t, TG)
                pe.wait_ge(s["xtl_done"], grp // 2 + 1)
                if t < TG:
                    b_ = bank[t % 2]
                    pe.wait_ge(set_done[M0 + pair // 2], 1)
                    if t >= 2:
                        pe.wait_ge(s["tl_done"], t - 1)
                else:
                    b_ = bank[T_BANK]
                    pe.wait_ge(s["tl_done"], t)
                c = slice(grp * GB * P, (grp + 1) * GB * P)
                for j in range(2):
                    h = 2 * pair + j
                    ins = split_mm(b_[:, GB * P * j:GB * P * (j + 1)], Mh[:, h, :], Ml[:, h, :], XTh[:, c], XTl[:, c])
                ins.then_inc(s["t_full"], 1)

            def x_item(n, x):
                if (b := due(x, UB, UB, B)) is not None:
                    pe.wait_ge(s["maxx_done"], UB * (b + 1))
                    if b:
                        pe.wait_ge(s["mxr_done"], b)
                    pe.wait_ge(s["qt_done"], sum(q_step(i) <= n for i in range(B)))
                    x2_before = sum(UB * i + X2T < x for i in range(B))
                    if x2_before:
                        pe.wait_ge(s["x2l_done"], x2_before)
                        if x2_before // GB:
                            pe.wait_ge(s["router_read"], x2_before // GB)
                    turn(MX_T, NMX2[:, b % 2, :], ID[:, :]).then_inc(s["mt_full"], 1)
                if 0 <= x < NU:
                    b, u = unit(x)
                    c = slice(b * P, (b + 1) * P)
                    if x == 0:
                        pe.wait_ge(s["kp_in"], 16 * (3 + B))
                        pe.wait_ge(s["one_rows"], 16)
                        pe.wait_ge(set_done[15], 1)
                    else:
                        pe.wait_ge(s["maxx_done"], x)
                    pe.wait_ge(q_in[b], 16)
                    for j in range(HU):
                        h = HU * u + j
                        ins = mm(bank[SX_BANK][:, j * P:(j + 1) * P], QP[0:KMAX, h, c], KP[0:KMAX, h, c], start=True, stop=True)
                    ins.then_inc(s["sx_full"], 1)
                m = x - ST_LAG
                if 0 <= m < NU:
                    b, u = unit(m)
                    c = slice(b * P, (b + 1) * P)
                    if m < 2:
                        pe.wait_ge(s["exp_done"], NU - 1 + m)
                    else:
                        pe.wait_ge(s["e32_done"], m - 1)
                    pe.wait_ge(m_in[b], 16)
                    for j in range(HU):
                        h = HU * u + j
                        ins = mm(bank[ST_BANK[m % 2]][:, j * P:(j + 1) * P], KP[0:KALL, h, c], QP[0:KALL, h, c], start=True, stop=True)
                    ins.then_inc(s["st_full"], 1)
                m = x - PX_LAG
                if 0 <= m < NU:
                    b, u = unit(m)
                    pe.wait_ge(s["el_done"], m + 1)
                    if u == 0:
                        pe.wait_ge(s["vparts_ready"], b + 1)
                        if b:
                            pe.wait_ge(s["px_read"], b)
                        else:
                            pe.wait_ge(s["pt_done"], NU)
                    for j in range(HU):
                        h = HU * u + j
                        to = bank[PX_BANK][:, h * VC:(h + 1) * VC]
                        mm(to, EH[:, m % 4, j * P:(j + 1) * P], XV[:, b, h, :], start=True, stop=False)
                        ins = mm(to, EL[:, m % 4, j * P:(j + 1) * P], XV[:, b, h, :], start=False, stop=True)
                    ins.then_inc(s["px_full"], 1)
                if (b := due(x, X2T, UB, B)) is not None:
                    pe.wait_ge(s["x2_normed"], b + 1)
                    pe.wait_ge(s["mxr_done"], sum(UB * (i + 1) <= x for i in range(B)))
                    if b:
                        pe.wait_ge(s["x2l_done"], b)
                        if b // GB:
                            pe.wait_ge(s["router_read"], b // GB)
                    else:
                        pe.wait_ge(s["qt_done"], B)
                    turn(TURNED, X2[:, b, :], ID[:, :]).then_inc(s["x2t_full"], 1)
                if (b := due(x, X2T + 2, UB, B)) is not None:
                    grp, half = divmod(b, GB)
                    pe.wait_ge(s["x2l_done"], b + 1)
                    pe.wait_ge(s["rw_split"], 2)
                    if grp:
                        pe.wait_ge(s["router_read"], grp)
                    c = slice(half * P, (half + 1) * P)
                    split_mm(ROUTER[:, half * E:(half + 1) * E], X2Th[:, grp, c], X2Tl[:, grp, c],
                             RWh[:, :], RWl[:, :]).then_inc(s["router_full"], 1)

            def expert_in(f, gu):
                grp, e = divmod(f, E)
                if e == 0:
                    pe.wait_ge(s["x2l_done"], GB * (grp + 1))
                if f == 0:
                    pe.wait_ge(s["w_done"], 3 * UB)
                    pe.wait_ge(s["v_done"], NU)
                else:
                    pe.wait_ge(s["hu_done" if gu else "gated"], f)
                for i in range(2):
                    ic = slice(i * P, (i + 1) * P)
                    ins = split_mm(bank[(G_BANK, U_BANK)[gu]][:, i * GB * P:(i + 1) * GB * P], WH[gu][:, e, ic],
                                   WL[gu][:, e, ic], X2Th[:, grp, :], X2Tl[:, grp, :])
                ins.then_inc(s["u_full" if gu else "g_full"], 1)

            pe.wait_ge(s["wk_in"], 16)
            for i in range(2):
                transposes(K0 + i, lambda j: WK[:, (4 * i + j) * P:(4 * i + j + 1) * P])
            pe.wait_ge(s["wq_in"], 16)
            for i in range(2):
                transposes(Q0 + i, lambda j: WQ[:, (4 * i + j) * P:(4 * i + j + 1) * P])
            for i in range(2):
                pe.wait_ge(s["xhat_done"], 4 * i + 4)
                transposes(X0 + i, lambda j: XHAT[:, 4 * i + j, :])
            for i in (K0, K0 + 1, Q0, Q0 + 1):
                pe.wait_ge(set_done[i], 1)
            for i in range(4):
                weight_product(M0, i, WKT, WQBD)
            pe.wait_ge(s["wv_in"], 16)
            for i in range(2):
                transposes(WV0 + i, lambda j: WV[:, (4 * i + j) * P:(4 * i + j + 1) * P])
            for i in range(4):
                t_product(2 * i)
                t_product(2 * i + 1)
                if i == 0:
                    pe.wait_ge(s["wo_in"], 32)
                    pe.wait_ge(set_done[WV0], 1)
                    pe.wait_ge(set_done[WV0 + 1], 1)
                weight_product(O0, i, WVT, WOBD)

            for n in range(STEPS):
                if n < NU:
                    b, u = unit(n)
                    c = slice(b * P, (b + 1) * P)
                    grp = b // GB
                    if n < 2:
                        pe.wait_ge(set_done[12 + n], 1)
                    else:
                        pe.wait_ge(s["exp_done"], n - 1)
                    pe.wait_ge(s["tl_done"], TG * grp + 2 * u + 2)
                    t_of = lambda T: T[:, grp % 2, b % GB, HU * u:HU * u + HU, :].rearrange("d h k -> d (h k)")
                    split_mm(bank[S_BANK[n % 2]][:, :], XTh[:, c], XTl[:, c], t_of(Th), t_of(Tl)).then_inc(s["s_full"], 1)
                if n + TG < NT:
                    t_product(n + TG)
                k = n - PT_LAG
                if 0 <= k < NU:
                    b, u = unit(k)
                    c = slice(b * P, (b + 1) * P)
                    if k == 0:
                        pe.wait_ge(s["tl_done"], TG)
                    else:
                        pe.wait_ge(s["v_done"], k)
                    pe.wait_ge(set_done[O0 + u], 1)
                    v_of = lambda V: V[:, HU * u:HU * u + HU, :].rearrange("d h n -> d (h n)")
                    split_mm(bank[V_BANK][:, :], XTh[:, c], XTl[:, c], v_of(Vh), v_of(Vl)).then_inc(s["v_full"], 1)
                    pe.wait_ge(s["p_norm"], k + 1)
                    if k:
                        pe.wait_ge(s["pt_done"], k)
                    else:
                        pe.wait_ge(set_done[14], 1)
                    for j in range(HU):
                        ins = turn(bank[PT_BANK][:, j * P:(j + 1) * P], EX[:, k % 3, j * P:(j + 1) * P], ID[:, :])
                    ins.then_inc(s["pt_full"], 1)
                k = n - PV_LAG
                if 0 <= k < NU:
                    b, u = unit(k)
                    pe.wait_ge(s["pt_done"], k + 1)
                    pe.wait_ge(s["v_done"], k + 1)
                    if u == 0 and b:
                        pe.wait_ge(s["y_added"], b)
                    for j in range(HU):
                        ins = mm(bank[ACC][:, 0:D], PTs[:, k % 3, j * P:(j + 1) * P], VP[:, k % 3, j * D:(j + 1) * D],
                                 start=u == 0 and j == 0, stop=u == UB - 1 and j == HU - 1)
                    ins.then_inc(s["pv_full"], 1)
                if (w := due(n, W0, 1, 3 * UB)) is not None:
                    if w == 0:
                        pe.wait_ge(s["tl_done"], NT)
                    else:
                        pe.wait_ge(s["w_done"], w)
                    pe.wait_ge(s[("gate_in", "up_in", "down_in")[w // 4]], 16)
                    for j in range(4):
                        if w < 8:
                            src = (GRAW if w < 4 else URAW)[:, 4 * (w % 4) + j, :]
                        else:
                            src = DRAW[:, 2 * (w - 8) + j // 2, j % 2, :]
                        ins = turn(bank[T_BANK][:, j * P:(j + 1) * P], src, ID[:, :])
                    ins.then_inc(s["w_full"], 1)
                if (b := due(n, k_step(0), 2, B)) is not None:
                    if b:
                        pe.wait_ge(s["kr_done"], b)
                    else:
                        pe.wait_ge(s["ck_turned"], 1)
                    q_before = sum(q_step(i) < n for i in range(B))
                    if q_before:
                        pe.wait_ge(s["qt_done"], q_before)
                    turn(TURNED, CKT[:, b, :], ID[:, :]).then_inc(s["kt_full"], 1)
                if (b := due(n, q_step(0), UB, B)) is not None:
                    pe.wait_ge(s["x_normed"], b + 1)
                    pe.wait_ge(s["kr_done"], sum(k_step(i) <= n for i in range(B)))
                    if b:
                        pe.wait_ge(s["qt_done"], b)
                    mx_before = sum(UB * (i + 1) < (x_items(n) or (0,))[0] for i in range(B))
                    if mx_before:
                        pe.wait_ge(s["mxr_done"], mx_before)
                    turn(TURNED, QTN[:, :], ID[:, :]).then_inc(s["qt_full"], 1)
                items = x_items(n)
                f = n - F0
                if 0 <= f < NF:
                    expert_in(f, 0)
                if items:
                    x_item(n, items[0])
                if 0 <= f < NF:
                    expert_in(f, 1)
                if items[1:]:
                    x_item(n, items[1])
                f = n - F0 - 1
                if 0 <= f < NF:
                    grp, e = divmod(f, E)
                    pe.wait_ge(s["hu_done"], f + 1)
                    if f:
                        pe.wait_ge(s["y_acc"], f)
                    else:
                        pe.wait_ge(s["y_added"], B)
                        pe.wait_ge(s["w_done"], 3 * UB)
                    for h2 in range(GB):
                        for i in range(2):
                            ins = mm(bank[Y_BANK][:, h2 * D:(h2 + 1) * D], HT[:, f % 2, i, h2 * P:(h2 + 1) * P], WD[:, e, i, :],
                                     start=i == 0, stop=i == 1)
                    ins.then_inc(s["dn_full"], 1)


_INS = ["x", "ctx_2048", "itok_Bx1_68_817", "L0_attn_ln_gamma", "L0_attn_ln_beta", "L0_attn_Wq", "L0_attn_Wk",
        "L0_attn_Wv", "L0_attn_Wo", "L0_xattn_b", "L0_ffn_router_w", "L0_ffn_gate_w", "L0_ffn_up_w", "L0_ffn_down_w"]


def kernel(**inputs):
    import numpy as np
    import concourse.bacc as bacc
    from concourse.bass_utils import run_bass_kernel_spmd

    nc = bacc.Bacc("TRN2", target_bir_lowering=False, num_devices=1)
    arrays, args = {}, []
    for name in _INS:
        a = np.ascontiguousarray(inputs[name])
        arrays[f"in_{name}"] = a
        args.append(nc.dram_tensor(f"in_{name}", a.shape, mybir.dt.from_np(a.dtype), kind="ExternalInput").ap())
    args.append(nc.dram_tensor("out_0", (B, P, D), F32, kind="ExternalOutput").ap())
    decoder_layer(nc, *args)
    r = run_bass_kernel_spmd(nc, [arrays], core_ids=[0])
    return r.results[0]["out_0"]
```

```python
from contextlib import ExitStack

import concourse.bass as bass
from concourse import mybir

F32 = mybir.dt.float32
F32R = mybir.dt.float32r
BF16 = mybir.dt.bfloat16
F16 = mybir.dt.float16
I32 = mybir.dt.int32
ALU = mybir.AluOpType
ACT = mybir.ActivationFunctionType
AX_X = mybir.AxisListType.X
SIZE = {F32: 4, F32R: 4, BF16: 2, F16: 2, I32: 4}

P = 128
B = 8
D = 128
H = 16
DH = 64
HU = 4
UB = H // HU
NU = B * UB
GB = 2
NG = B // GB
TG = H // 2
NT = NG * TG
XH = D // H
PARTS = 3
KROWS = PARTS * PARTS * XH
KMAX = KROWS + 2 * PARTS
KALL = KMAX + PARTS
VC = PARTS * XH + 1
EPS = 1e-5
E = 8
FI = 256
NTOK = B * P
NF = NG * E

PT_LAG, PV_LAG = 2, 3
TAIL = UB - 1 + PV_LAG
XLEAD = 2 * UB
XS = NU - XLEAD
ST_LAG = XLEAD
PX_LAG = ST_LAG + 2
XTAIL = UB - 1 + PX_LAG
X2T = XTAIL + 5
ROUTE = XTAIL + 8
SX_ALT = XLEAD + 2 * (TAIL - UB + 1)
SX_ONE = SX_ALT + 3 * UB
Y_ALT = UB + 2
EL_DVE = 4 * UB
W0 = NU - UB
F0 = NU + UB * 2
FAST = 4
STEPS = F0 + NF + 5
assert UB * (GB - 1) + X2T + 1 < XLEAD + 2 * (F0 - NU)


def x_items(n):
    if n < XS:
        return ()
    if n < NU:
        return (n - XS,)
    if n < F0 + FAST:
        return (XLEAD + 2 * (n - NU), XLEAD + 2 * (n - NU) + 1)
    return (XLEAD + 2 * (F0 + FAST - NU) + n - F0 - FAST,)


def mask_parts():
    import numpy as np
    rest, out = np.float32(-1e12), []
    for _ in range(PARTS):
        top = np.array([rest], np.float32).view(np.uint32) & np.uint32(0xFFFF0000)
        out.append(float(top.view(np.float32)[0]))
        rest = np.float32(rest - np.float32(out[-1]))
    assert rest == 0
    return out


def decoder_layer(nc, x_in, ctx_in, seq_len, gamma, beta, wq, wk, wv, wo, key_bias, router_w, gate_w, up_w,
                  down_w, out):
    stack = ExitStack()
    with stack:
        sem = lambda name: stack.enter_context(nc.semaphore(name))
        KB = 1024
        base = (nc.sbuf_base + 63) // 64 * 64
        ARENA = 207 * KB
        stack.enter_context(nc.sbuf_tensor("arena", [P, ARENA // 4 + 16], F32))

        def at(name, kb, shape, dt=F32):
            n = SIZE[dt]
            for size in shape[1:]:
                n *= size
            assert kb * KB + n <= ARENA, name
            return nc.alloc_sbuf_tensor_at(name, shape, dt, offset=base + int(kb * KB))

        def shelf(kb, end):
            cur = [kb * KB]

            def put(name, shape, dt=F32):
                n = SIZE[dt]
                for size in shape[1:]:
                    n *= size
                t = nc.alloc_sbuf_tensor_at(name, shape, dt, offset=base + cur[0])
                cur[0] += (n + 31) // 32 * 32
                assert cur[0] <= end * KB, name
                return t
            return put

        X = at("X", 0, [P, B, D])
        X2 = at("X2", 0, [P, B, D])
        X1 = at("X1", 4, [P, B, D])
        XTh = at("XTh", 8, [D, NTOK], F32R)
        XTl = at("XTl", 12, [D, NTOK], F32R)
        CV = at("CV", 16, [P, B, D])
        QP = at("QP", 20, [P, H, NTOK], BF16)
        KP = at("KP", 52, [P, H, NTOK], BF16)
        Mh = at("Mh", 84, [D, H, D], F32R)
        Ml = at("Ml", 92, [D, H, D], F32R)
        Vh = at("Vh", 100, [D, H, D], F32R)
        Vl = at("Vl", 108, [D, H, D], F32R)
        Th = at("Th", 116, [D, 2, GB, H, P], F32R)
        Tl = at("Tl", 148, [D, 2, GB, H, P], F32R)
        VP = at("VP", 180, [P, 3, HU * D])
        EX = at("EX", 186, [P, 3, HU * P])
        PTs = at("PTs", 192, [P, 3, HU * P])
        WK = at("WK", 132, [P, H * DH])
        WQ = at("WQ", 136, [P, H * DH])
        WV = at("WV", 140, [P, H * DH])
        WKT = at("WKT", 144, [P, 8, D])
        WVT = at("WVT", 164, [P, 8, D])
        WQBD = at("WQBD", 168, [P, 8, 2, D])
        WOBD = at("WOBD", 186, [P, 8, 2, D])
        XHAT = at("XHAT", 20, [P, B, D])
        XTF = at("XTF", 24, [D, NTOK])
        put = shelf(52, 84)
        CK = put("CK", [P, B, D])
        CKT = put("CKT", [P, B, D])
        KR = put("KR", [D, P])
        KT = put("KT", [D, 2, PARTS, P], BF16)
        BROW = put("BROW", [1, P])
        BRES = put("BRES", [1, P])
        BPT = put("BPT", [1, PARTS, P], BF16)
        SLI = put("SLI", [B, 1], I32)
        SLF = put("SLF", [B, 1])
        KIX = put("KIX", [B, P])
        MPT = put("MPT", [B, PARTS, P], BF16)
        put = shelf(116, 132)
        XV = put("XV", [P, B, H, VC], BF16)
        E32 = put("E32", [P, 2, HU * P])
        PXS = put("PXS", [P, 2, H, VC])
        NMX2 = put("NMX2", [P, 2, H])
        MXT = put("MXT", [H, 2, PARTS, P], BF16)
        MR = put("MR", [H, P])
        WTE = put("WTE", [P, GB, E])
        EH = at("EH", 172, [P, 4, HU * P], F16)
        EL = at("EL", 176, [P, 4, HU * P], F16)
        WH = [at("WGh", 148, [D, E, FI], F32R), at("WUh", 132, [D, E, FI], F32R)]
        WL = [at("WGl", 156, [D, E, FI], F32R), at("WUl", 140, [D, E, FI], F32R)]
        WD = at("WD", 164, [P, E, 2, D])
        GRAW = at("GRAW", 84, [P, 2 * E, D])
        URAW = at("URAW", 92, [P, 2 * E, D])
        DRAW = at("DRAW", 100, [P, E, 2, P])
        X2Th = at("X2Th", 84, [D, NG, GB * P], F32R)
        X2Tl = at("X2Tl", 88, [D, NG, GB * P], F32R)
        SG = at("SG", 92, [P, 2, 2, GB * P])
        HT = at("HT", 96, [P, 2, 2, GB * P])
        Z = at("Z", 100, [P, B, D])
        OUT = at("OUT", 104, [P, B, D])
        put = shelf(108, 116)
        LG, PR, EQ, HOT1, HOT2, WT = (put(n, [P, NG, GB, E]) for n in ("LG", "PR", "EQ", "HOT1", "HOT2", "WT"))
        ROWS = put("ROWS", [P, 8, GB])
        NUM = put("NUM", [P, D])
        WY = put("WY", [P, 2, GB * D])
        XR = put("XR", [P, H])
        put = shelf(198, 207)
        ID = put("ID", [P, P])
        ONES = put("ONES", [P, P], BF16)
        Y = put("Y", [P, 2, D])
        QT = put("QT", [P, 2, PARTS, P], BF16)
        QR = put("QR", [D, P])
        QTN = put("QTN", [P, D])
        GBC = put("GBC", [P, 2])
        HALF = put("HALF", [P, B])
        NMX = put("NMX", [P, 4, HU])
        SUM = put("SUM", [P, 4, HU])
        RCP = put("RCP", [P, 4, HU])
        BST = put("BST", [P, B, 6])
        BMV = put("BMV", [P, B, 2])
        VE = put("VE", [P, B])
        RS = put("RS", [P, B])
        TST = put("TST", [P, 6])
        TMV = put("TMV", [P, 2, 2])
        TVE = put("TVE", [P, 2])
        TRS = put("TRS", [P, 2])
        RW = put("RW", [D, E])
        RWh = put("RWh", [D, E], F32R)
        RWl = put("RWl", [D, E], F32R)

        bank = [stack.enter_context(nc.psum_tensor(f"bank{i}", [P, 512], F32)) for i in range(8)]
        T_BANK, V_BANK, S_BANK, PT_BANK, ACC = 0, 1, (2, 3), 4, 6
        G_BANK, U_BANK, ST_BANK, PX_BANK, SX_BANK, Y_BANK = 0, 1, (2, 3), 4, 5, 6
        y_bank = lambda f: bank[SX_BANK] if f >= Y_ALT and f % 2 else bank[Y_BANK]
        sx_bank = lambda x: bank[Y_BANK] if SX_ALT <= x < SX_ONE and x % 2 else bank[SX_BANK]
        TURNED = bank[7][:, 0:P]
        MX_T = bank[7][0:H, P:2 * P]
        ROUTER = bank[7][:, 2 * P:2 * P + GB * E]

        dram = lambda name, shape, dt: nc.dram_tensor(name, shape, dt, kind="Internal").ap()
        k_rows = dram("k_rows", [PARTS, PARTS, XH * H, NTOK], BF16)
        q_rows = dram("q_rows", [B, PARTS, PARTS, XH * H, P], BF16)
        bias_rows = dram("bias_rows", [PARTS, P], BF16)
        mask_rows = dram("mask_rows", [B, PARTS, P], BF16)

        names = """x_in wq_in wv_in wo_in gb_in ck_in cv_in rw_in rows_in gate_in up_in down_in
            ident zeroed ones_ready consts stats_x rstd_x xhat_done dve_link pool_link setup_full xtf_done
            xth_done xtl_done mh_done oh_done t_full th_done tl_done s_full max_done exp_done sum_recip
            p_norm v_full v_done px_read sums_added pt_full pt_done pv_full y_added var_ready rstd_ready
            x_normed kt_full kh_done kr_done kt_done qh_done ck_turned q_read rows_ready rows_out kp_in
            one_rows qt_full qt_done sx_full maxx_done mt_full mxh_done mxr_done mt_done st_full e32_done
            el_pool el_dve px_full num_done x2_normed x2t_full x2h_done x2l_done rw_split router_full
            router_read route_exp weights_ready vparts_ready w_full wh_done w_done g_full u_full tanh_done
            gated hu_done dn_full y_read y_acc last_var last_rstd out_ready stored""".split()
        s = {n: sem(n) for n in names}
        set_done = [sem(f"setup_done{i}") for i in range(16)]
        wk_in = [sem(f"wk_in{i}") for i in range(2)]
        q_out = [sem(f"q_out{b}") for b in range(B)]
        q_in = [sem(f"q_in{b}") for b in range(B)]
        m_in = [sem(f"m_in{b}") for b in range(B)]
        k_out = [sem(f"k_out{i}") for i in range(2)]
        block = stack.enter_context(nc.Block())

        K0, Q0, X0, M0, WV0, O0 = 0, 2, 4, 6, 10, 12
        sbank = lambda i: bank[2 + i % 4]
        unit = lambda n: (n // UB, n % UB)

        def due(n, first, every, count):
            i, off = divmod(n - first, every)
            return i if off == 0 and 0 <= i < count else None

        k_step = lambda b: 2 * b + 3
        q_step = lambda b: UB * b + TAIL + 2

        by_dve = lambda m: m < EL_DVE and m % 2 == 1

        def el_done(m):
            mine = by_dve(m)
            return s["el_dve" if mine else "el_pool"], sum(by_dve(i) == mine for i in range(m + 1))

        @block.sync
        def _(sp):
            sp.dma_start(X[:, :, :], x_in.rearrange("b s d -> s b d")).then_inc(s["x_in"], 16)
            sp.dma_start(WQ[:, :], wq).then_inc(s["wq_in"], 16)
            sp.dma_start(WV[:, :], wv).then_inc(s["wv_in"], 16)
            sp.wait_ge(s["zeroed"], 2)
            for j in range(2):
                sp.dma_start(WOBD[DH * j:DH * j + DH, :, j, :],
                             wo.rearrange("(c j p) n -> j p c n", j=2, p=DH)[j]).then_inc(s["wo_in"], 16)
            sp.dma_start(CK[:, :, :], ctx_in[:, :, 0:D].rearrange("b s d -> s b d")).then_inc(s["ck_in"], 16)
            sp.dma_start(BROW[:, :], key_bias.rearrange("(a k) -> a k", a=1)).then_inc(s["rows_in"], 16)
            sp.dma_start(SLI[:, :], seq_len).then_inc(s["rows_in"], 16)
            sp.dma_start(CV[:, :, :], ctx_in[:, :, D:2 * D].rearrange("b s d -> s b d")).then_inc(s["cv_in"], 16)
            sp.wait_ge(s["rows_ready"], 1)
            sp.dma_start(bias_rows.rearrange("(a p) k -> a p k", a=1), BPT[:, :, :]).then_inc(s["rows_out"], 16)
            sp.dma_start(mask_rows, MPT[:, :, :]).then_inc(s["rows_out"], 16)

            def keys_out(b):
                sp.wait_ge(s["kt_done"], b + 1)
                for i in range(PARTS):
                    sp.dma_start(k_rows[i].rearrange("j r k -> r j k")[:, :, b * P:(b + 1) * P],
                                 KT[:, b % 2, :, :]).then_inc(k_out[b % 2], 16)

            def queries(b):
                sp.wait_ge(s["qt_done"], b + 1)
                for j in range(PARTS):
                    sp.dma_start(q_rows[b].rearrange("i j r q -> j r i q")[j], QT[:, b % 2, :, :]).then_inc(q_out[b], 16)
                sp.wait_ge(q_out[b], 16 * PARTS)
                sp.dma_start(QP[0:KROWS, :, b * P:(b + 1) * P],
                             q_rows[b].rearrange("i j (d h) q -> (i j d) h q", h=H)).then_inc(q_in[b], 16)

            def keys_in():
                for i in range(2):
                    sp.wait_ge(k_out[i], 16 * PARTS * B // 2)
                sp.wait_ge(s["rows_out"], 32)
                sp.dma_start(KP[0:KROWS, :, :],
                             k_rows.rearrange("i j (d h) k -> (i j d) h k", h=H)).then_inc(s["kp_in"], 16)
                sp.dma_start(KP[KROWS:KROWS + PARTS, :, :].rearrange("r h (b k) -> r (h b) k", k=P),
                             bias_rows[:, None, :].broadcast_to([PARTS, H * B, P])).then_inc(s["kp_in"], 16)
                for b in range(B):
                    sp.dma_start(KP[KROWS + PARTS:KMAX, :, b * P:(b + 1) * P],
                                 mask_rows[b, :, None, :].broadcast_to([PARTS, H, P])).then_inc(s["kp_in"], 16)
                sp.dma_start(KP[KMAX:KALL, :, :].rearrange("r h (b k) -> r (h b) k", k=P),
                             ONES[0:PARTS, None, :].broadcast_to([PARTS, H * B, P])).then_inc(s["kp_in"], 16)

            sp.wait_ge(s["ones_ready"], 1)
            sp.wait_ge(s["xtl_done"], 2)
            sp.dma_start(QP[KROWS:KMAX, :, :].rearrange("r h (b q) -> r (h b) q", q=P),
                         ONES[0:KMAX - KROWS, None, :].broadcast_to([KMAX - KROWS, H * B, P])).then_inc(s["one_rows"], 16)
            for n in range(STEPS):
                if (b := due(n, k_step(0), 2, B)) is not None:
                    keys_out(b)
                    if b == B - 1:
                        keys_in()
                if (b := due(n, q_step(0), UB, B)) is not None:
                    queries(b)
                if n == TG * (NG - 1):
                    sp.wait_ge(s["t_full"], NT)
                    sp.dma_start(GRAW[:, :, :], gate_w.rearrange("e (c p) h -> p (e c) h", p=P)).then_inc(s["gate_in"], 16)
                    sp.dma_start(URAW[:, :, :], up_w.rearrange("e (c p) h -> p (e c) h", p=P)).then_inc(s["up_in"], 16)
                if n == NU + 2:
                    sp.wait_ge(s["v_full"], NU)
                    sp.dma_start(DRAW[:, :, :, :], down_w.rearrange("e h (c i) -> h e c i", c=2)).then_inc(s["down_in"], 16)
                for x in x_items(n):
                    if (b := due(x, UB, UB, B)) is not None:
                        sp.wait_ge(s["mt_done"], b + 1)
                        for p in range(PARTS):
                            sp.dma_start(QP[KMAX + p:KMAX + p + 1, :, b * P:(b + 1) * P],
                                         MXT[0:H, b % 2, p, :]).then_inc(m_in[b], 16)
                if (grp := due(n, F0 + E + 3, E, NG)) is not None:
                    for b in range(GB * grp, GB * grp + GB):
                        sp.wait_ge(s["out_ready"], b + 1)
                        sp.dma_start(out[b], OUT[:, b, :]).then_inc(s["stored"], 16)
            sp.wait_ge(s["stored"], 16 * B)

        @block.gpsimd
        def _(pool):
            g = nc.gpsimd
            chain = [0]

            def link(ins):
                chain[0] += 1
                ins.then_inc(s["pool_link"], 1)
                pool.wait_ge(s["pool_link"], chain[0])

            link(g.memset(ID[:, :], 0.0))
            g.affine_select(out=ID[:, :], in_=ID[:, :], compare_op=ALU.not_equal, fill=1.0, base=0,
                            pattern=[[-1, P]], channel_multiplier=1).then_inc(s["ident"], 1)
            link(g.memset(HALF[:, :], -0.5))
            g.memset(WQBD[:, :, :, :], 0.0).then_inc(s["zeroed"], 1)
            pool.wait_ge(s["stats_x"], 1)
            g.tensor_tensor(RS[:, :], VE[:, :], HALF[:, :], ALU.pow).then_inc(s["rstd_x"], 1)
            g.memset(WOBD[:, :, :, :], 0.0).then_inc(s["zeroed"], 1)
            g.memset(ONES[:, :], 1.0).then_inc(s["ones_ready"], 1)
            pool.wait_ge(s["rows_in"], 32)
            link(g.iota(KIX[:, :], pattern=[[1, P]], base=0, channel_multiplier=0,
                        allow_small_or_imprecise_dtypes=True))
            link(g.tensor_copy(SLF[:, :], SLI[:, :]))
            for p, c in enumerate(mask_parts()):
                link(g.tensor_scalar(MPT[:, p, :], KIX[:, :], SLF[:, 0:1], c, ALU.is_ge, ALU.mult))
            link(g.tensor_copy(BPT[:, 0, :], BROW[:, :]))
            link(g.tensor_tensor(BRES[:, :], BROW[:, :], BPT[:, 0, :], ALU.subtract))
            link(g.tensor_copy(BPT[:, 1, :], BRES[:, :]))
            link(g.tensor_tensor(BRES[:, :], BRES[:, :], BPT[:, 1, :], ALU.subtract))
            g.tensor_copy(BPT[:, 2, :], BRES[:, :]).then_inc(s["rows_ready"], 1)
            pool.wait_ge(s["rows_ready"], 1)

            def deviation(i):
                pool.wait_ge(s["var_ready"], i + 1)
                g.tensor_tensor(TRS[:, i % 2:i % 2 + 1], TVE[:, i % 2:i % 2 + 1], HALF[:, 0:1],
                                ALU.pow).then_inc(s["rstd_ready"], 1)

            for n in range(STEPS):
                if (b := due(n, TAIL, UB, B)) is not None:
                    deviation(b)
                if n < NU:
                    pool.wait_ge(s["sum_recip"], n + 1)
                    e = EX[:, n % 3, :].rearrange("q (h k) -> q h k", h=HU)
                    g.tensor_tensor(e, e, RCP[:, n % 4, :, None].broadcast_to([P, HU, P]),
                                    ALU.mult).then_inc(s["p_norm"], 1)
                if (b := due(n, k_step(0), 2, B)) is not None:
                    pool.wait_ge(s["kr_done"], b + 1)
                    link(g.tensor_copy(KT[:, b % 2, 1, :], KR[:, :]))
                    g.tensor_tensor(KT[:, b % 2, 2, :], KR[:, :], KT[:, b % 2, 1, :],
                                    ALU.subtract).then_inc(s["kt_done"], 1)
                if n == XS:
                    pool.wait_ge(s["s_full"], TG * (NG - 1))
                    g.memset(XV[:, :, :, VC - 1:VC].rearrange("k b h c -> k (b h) c"), 1.0)
                    g.iota(WTE[:, :, :], pattern=[[0, GB], [-1, E]], base=E, channel_multiplier=0,
                           allow_small_or_imprecise_dtypes=True).then_inc(s["consts"], 1)
                if (b := due(n, XS + 1, 1, B)) is not None:
                    if b == 0:
                        pool.wait_ge(s["cv_in"], 16)
                    src = CV[:, b, :].rearrange("k (h d) -> k h d", h=H)
                    part = lambda p: XV[:, b, :, p * XH:(p + 1) * XH]
                    link(g.tensor_copy(part(0), src))
                    link(g.tensor_tensor(src, src, part(0), ALU.subtract))
                    link(g.tensor_copy(part(1), src))
                    g.tensor_tensor(part(2), src, part(1), ALU.subtract).then_inc(s["vparts_ready"], 1)
                f = n - F0 - 2
                if 0 <= f < NF:
                    grp, e = divmod(f, E)
                    pool.wait_ge(s["y_read"], f + 1)
                    if e:
                        pool.wait_ge(s["y_acc"], f)
                    bs = slice(GB * grp, GB * grp + GB)
                    g.tensor_tensor(Z[:, bs, :], WY[:, f % 2, :].rearrange("t (b h) -> t b h", b=GB),
                                    (Z if e else X2)[:, bs, :], ALU.add).then_inc(s["y_acc"], 1)
                for x in x_items(n):
                    if (b := due(x, UB, UB, B)) is not None:
                        pool.wait_ge(s["mxr_done"], b + 1)
                        link(g.tensor_copy(MXT[:, b % 2, 1, :], MR[:, :]))
                        g.tensor_tensor(MXT[:, b % 2, 2, :], MR[:, :], MXT[:, b % 2, 1, :],
                                        ALU.subtract).then_inc(s["mt_done"], 1)
                    m = x - ST_LAG
                    if 0 <= m < NU and not by_dve(m):
                        pool.wait_ge(s["e32_done"], m + 1)
                        if m >= 4:
                            pool.wait_ge(s["px_full"], m - 3)
                        g.tensor_tensor(EL[:, m % 4, :], E32[:, m % 2, :], EH[:, m % 4, :],
                                        ALU.subtract).then_inc(s["el_pool"], 1)
                    if (b := due(x, XTAIL, UB, B)) is not None:
                        pool.wait_ge(s["px_read"], b + 1)
                        part = lambda p: PXS[:, b % 2, :, p * XH:(p + 1) * XH]
                        num = NUM[:, :].rearrange("q (h d) -> q h d", h=H)
                        if b:
                            pool.wait_ge(s["sums_added"], b)
                        link(g.tensor_tensor(num, part(1), part(2), ALU.add))
                        link(g.tensor_tensor(num, num, part(0), ALU.add))
                    if (b := due(x, XTAIL + 1, UB, B)) is not None:
                        num = NUM[:, :].rearrange("q (h d) -> q h d", h=H)
                        pool.wait_ge(s["num_done"], b + 1)
                        link(g.tensor_tensor(num, num, XR[:, :, None].broadcast_to([P, H, XH]), ALU.mult))
                        pool.wait_ge(s["x_normed"], B)
                        if b >= 2:
                            pool.wait_ge(s["x2_normed"], b - 1)
                        g.tensor_tensor(Y[:, b % 2, :], NUM[:, :], X1[:, b, :], ALU.add).then_inc(s["sums_added"], 1)
                    if (b := due(x, XTAIL + 3, UB, B)) is not None:
                        deviation(B + b)
                if (grp := due(n, F0 + E + 2, E, NG)) is not None:
                    pool.wait_ge(s["last_var"], grp + 1)
                    gb = slice(GB * grp, GB * grp + GB)
                    g.tensor_tensor(RS[:, gb], VE[:, gb], HALF[:, gb], ALU.pow).then_inc(s["last_rstd"], 1)

        @block.scalar
        def _(act):
            a = nc.scalar
            for i in range(2):
                act.dma_start(WK[:, 512 * i:512 * i + 512], wk[:, 512 * i:512 * i + 512]).then_inc(wk_in[i], 16)
            act.dma_start(GBC[:, 0:1], gamma.rearrange("(d a) -> d a", a=1)).then_inc(s["gb_in"], 16)
            act.dma_start(GBC[:, 1:2], beta.rearrange("(d a) -> d a", a=1)).then_inc(s["gb_in"], 16)
            act.dma_start(RW[:, :], router_w.rearrange("e h -> h e"),
                          allow_slow_non_contiguous=True).then_inc(s["rw_in"], 16)

            def setup(i, out_ap, then):
                act.wait_ge(s["setup_full"], i + 1)
                a.activation(out_ap, sbank(i)[:, :], ACT.Copy).then_inc(then, 1)

            def t_high(t):
                grp, pair = divmod(t, TG)
                act.wait_ge(s["t_full"], t + 1)
                b_ = bank[t % 2] if t < TG else bank[T_BANK]
                a.activation(Th[:, grp % 2, :, 2 * pair:2 * pair + 2, :].rearrange("d b h k -> d h b k"),
                             b_[:, :].rearrange("d (h b k) -> d h b k", h=2, b=GB), ACT.Copy).then_inc(s["th_done"], 1)

            for i in range(2):
                setup(K0 + i, WKT[:, 4 * i:4 * i + 4, :], set_done[K0 + i])
            act.wait_ge(s["zeroed"], 1)
            for i in range(2):
                act.wait_ge(s["setup_full"], Q0 + i + 1)
                for j in range(2):
                    ins = a.activation(WQBD[DH * j:DH * j + DH, 4 * i:4 * i + 4, j, :],
                                       sbank(Q0 + i)[DH * j:DH * j + DH, :].rearrange("p (c d) -> p c d", c=4),
                                       ACT.Copy, scale=float(DH) ** -0.5)
                ins.then_inc(set_done[Q0 + i], 1)
            for i in range(2):
                act.wait_ge(s["xtf_done"], i + 1)
                c = slice(512 * i, 512 * i + 512)
                a.activation(XTh[:, c], XTF[:, c], ACT.Copy).then_inc(s["xth_done"], 1)
            for i in range(4):
                setup(M0 + i, Mh[:, 4 * i:4 * i + 4, :], s["mh_done"])
            for i in range(2):
                setup(WV0 + i, WVT[:, 4 * i:4 * i + 4, :], set_done[WV0 + i])
            for i in range(4):
                t_high(2 * i)
                t_high(2 * i + 1)
                if i < 2:
                    setup(O0 + i, Vh[:, 4 * i:4 * i + 4, :], s["oh_done"])

            def maxima_high(x):
                if (b := due(x, UB, UB, B)) is not None:
                    act.wait_ge(s["mt_full"], b + 1)
                    if b >= 2:
                        act.wait_ge(m_in[b - 2], 16 * PARTS)
                    a.activation(MXT[:, b % 2, 0, :], MX_T, ACT.Copy).then_inc(s["mxh_done"], 1)

            for n in range(STEPS):
                if n + TG < NT:
                    t_high(n + TG)
                if n < 2:
                    setup(O0 + 2 + n, Vh[:, 8 + 4 * n:12 + 4 * n, :], s["oh_done"])
                if XS <= n < NU:
                    maxima_high(n - XS)
                if n < NU:
                    act.wait_ge(s["max_done"], n + 1)
                    if n >= 3:
                        act.wait_ge(s["pt_full"], n - 2)
                    for j in range(HU):
                        ins = a.activation(EX[:, n % 3, j * P:(j + 1) * P], bank[S_BANK[n % 2]][:, j * P:(j + 1) * P],
                                           ACT.Exp, bias=NMX[:, n % 4, j:j + 1], accum_out=SUM[:, n % 4, j:j + 1])
                    ins.then_inc(s["exp_done"], 1)
                k = n - PT_LAG
                if 0 <= k < NU:
                    act.wait_ge(s["v_full"], k + 1)
                    if k >= 3:
                        act.wait_ge(s["pv_full"], k - 2)
                    a.activation(VP[:, k % 3, :], bank[V_BANK][:, :], ACT.Copy).then_inc(s["v_done"], 1)
                if (b := due(n, k_step(0), 2, B)) is not None:
                    act.wait_ge(s["kt_full"], b + 1)
                    if b >= 2:
                        act.wait_ge(k_out[b % 2], 16 * PARTS * (b // 2))
                    a.activation(KT[:, b % 2, 0, :], TURNED, ACT.Copy).then_inc(s["kh_done"], 1)
                if (b := due(n, q_step(0), UB, B)) is not None:
                    act.wait_ge(s["qt_full"], b + 1)
                    if b >= 2:
                        act.wait_ge(q_out[b - 2], 16 * PARTS)
                    a.activation(QT[:, b % 2, 0, :], TURNED, ACT.Copy, scale=float(XH) ** -0.5).then_inc(s["qh_done"], 1)
                f = n - F0 - 2
                if 0 <= f < NF:
                    grp, e = divmod(f, E)
                    act.wait_ge(s["dn_full"], f + 1)
                    if e == 0:
                        act.wait_ge(s["weights_ready"], grp + 1)
                    if f >= 2:
                        act.wait_ge(s["y_acc"], f - 1)
                    for half in range(GB):
                        c = slice(half * D, (half + 1) * D)
                        ins = a.activation(WY[:, f % 2, c], y_bank(f)[:, c], ACT.Copy, scale=WT[:, grp, half, e:e + 1])
                    ins.then_inc(s["y_read"], 1)
                f = n - F0
                if 0 <= f < NF:
                    act.wait_ge(s["g_full"], f + 1)
                    if f >= 2:
                        act.wait_ge(s["hu_done"], f - 1)
                    a.activation(SG[:, f % 2, :, :].rearrange("i c t -> i (c t)"), bank[G_BANK][:, :],
                                 ACT.Tanh, scale=0.5).then_inc(s["tanh_done"], 1)
                for x in x_items(n):
                    if n >= NU:
                        maxima_high(x)
                    if (b := due(x, XTAIL, UB, B)) is not None:
                        act.wait_ge(s["px_full"], UB * b + UB)
                        if b >= 2:
                            act.wait_ge(s["sums_added"], b - 1)
                            act.wait_ge(s["num_done"], b - 1)
                        a.activation(PXS[:, b % 2, :, :].rearrange("q h c -> q (h c)"), bank[PX_BANK][:, 0:H * VC],
                                     ACT.Copy).then_inc(s["px_read"], 1)
                    m = x - ST_LAG
                    if 0 <= m < NU:
                        act.wait_ge(s["st_full"], m + 1)
                        if m >= 4:
                            act.wait_ge(s["px_full"], m - 3)
                        if m >= 2:
                            act.wait_ge(*el_done(m - 2))
                        if m == 0:
                            act.wait_ge(s["s_full"], NU)
                        a.activation(EH[:, m % 4, :], bank[ST_BANK[m % 2]][:, :], ACT.Exp)
                        a.activation(E32[:, m % 2, :], bank[ST_BANK[m % 2]][:, :], ACT.Exp).then_inc(s["e32_done"], 1)
                    if (b := due(x, X2T, UB, B)) is not None:
                        act.wait_ge(s["x2t_full"], b + 1)
                        grp, half = divmod(b, GB)
                        if b == 0:
                            act.wait_ge(s["w_full"], UB)
                        a.activation(X2Th[:, grp, half * P:(half + 1) * P], TURNED, ACT.Copy).then_inc(s["x2h_done"], 1)
                    if (grp := due(x, UB * (GB - 1) + ROUTE, UB * GB, NG)) is not None:
                        act.wait_ge(s["router_read"], grp + 1)
                        a.activation(PR[:, grp, :, :], LG[:, grp, :, :], ACT.Exp).then_inc(s["route_exp"], 1)
                    if x == x_items(n)[0] and (w := due(n, W0, 1, 3 * UB)) is not None:
                        act.wait_ge(s["w_full"], w + 1)
                        es = slice(2 * (w % 4), 2 * (w % 4) + 2)
                        if w < 8:
                            a.activation(WH[w // 4][:, es, :], bank[T_BANK][:, :].rearrange("h (e i) -> h e i", e=2),
                                         ACT.Copy).then_inc(s["wh_done"], 1)
                        else:
                            a.activation(WD[:, es, :, :], bank[T_BANK][:, :].rearrange("i (e c h) -> i e c h", e=2, c=2),
                                         ACT.Copy, scale=0.5).then_inc(s["w_done"], 1)

        @block.vector
        def _(dve):
            v = nc.vector
            chain = [0]

            def mark(ins):
                chain[0] += 1
                ins.then_inc(s["dve_link"], 1)

            def link(ins):
                mark(ins)
                dve.wait_ge(s["dve_link"], chain[0])

            dve.wait_ge(s["x_in"], 16)
            for b in range(B):
                ins = v.bn_stats(BST[:, b, :], X[:, b, :])
            link(ins)
            for b in range(B):
                ins = v.bn_aggr(BMV[:, b, :], BST[:, b, :])
            link(ins)
            v.tensor_scalar(VE[:, :], BMV[:, :, 1], EPS, None, ALU.add).then_inc(s["stats_x"], 1)
            dve.wait_ge(s["rstd_x"], 1)
            for b in range(B):
                v.tensor_scalar(XHAT[:, b, :], X[:, b, :], BMV[:, b, 0:1], RS[:, b:b + 1], ALU.subtract,
                                ALU.mult).then_inc(s["xhat_done"], 1)
            dve.wait_ge(s["gb_in"], 32)
            for i in range(2):
                c = slice(512 * i, 512 * i + 512)
                dve.wait_ge(s["setup_full"], X0 + i + 1)
                v.tensor_scalar(XTF[:, c], sbank(X0 + i)[:, :], GBC[:, 0:1], GBC[:, 1:2], ALU.mult,
                                ALU.add).then_inc(s["xtf_done"], 1)
            for i in range(2):
                c = slice(512 * i, 512 * i + 512)
                dve.wait_ge(s["xth_done"], i + 1)
                v.tensor_tensor(XTl[:, c], XTF[:, c], XTh[:, c].bitcast(F32), ALU.subtract).then_inc(s["xtl_done"], 1)

            def low_weights(i, item, high, low_):
                hs = slice(4 * i, 4 * i + 4)
                v.tensor_tensor(low_[:, hs, :], sbank(item)[:, :].rearrange("p (h d) -> p h d", h=4),
                                high[:, hs, :].bitcast(F32), ALU.subtract).then_inc(set_done[item], 1)

            def t_low(t):
                grp, pair = divmod(t, TG)
                dve.wait_ge(s["th_done"], t + 1)
                b_ = bank[t % 2] if t < TG else bank[T_BANK]
                to = lambda T: T[:, grp % 2, :, 2 * pair:2 * pair + 2, :].rearrange("d b h k -> d h b k")
                v.tensor_tensor(to(Tl), b_[:, :].rearrange("d (h b k) -> d h b k", h=2, b=GB), to(Th).bitcast(F32),
                                ALU.subtract).then_inc(s["tl_done"], 1)

            for i in range(4):
                dve.wait_ge(s["mh_done"], i + 1)
                low_weights(i, M0 + i, Mh, Ml)
            for i in range(4):
                t_low(2 * i)
                t_low(2 * i + 1)
                if i < 2:
                    dve.wait_ge(s["oh_done"], i + 1)
                    low_weights(i, O0 + i, Vh, Vl)
            dve.wait_ge(s["rw_in"], 16)
            v.tensor_copy(RWh[:, :], RW[:, :]).then_inc(s["rw_split"], 1)
            dve.wait_ge(s["rw_split"], 1)
            v.tensor_tensor(RWl[:, :], RW[:, :], RWh[:, :].bitcast(F32), ALU.subtract).then_inc(s["rw_split"], 1)

            dve.wait_ge(s["ck_in"], 16)
            v.tensor_copy(CKT[:, :, :].rearrange("k b (d h) -> k b h d", h=H),
                          CK[:, :, :].rearrange("k b (h d) -> k b h d", h=H)).then_inc(s["ck_turned"], 1)

            def statistics(i, y):
                link(v.bn_stats(TST[:, :], y))
                link(v.bn_aggr(TMV[:, i % 2, :], TST[:, :]))
                v.tensor_scalar(TVE[:, i % 2:i % 2 + 1], TMV[:, i % 2, 1:2], EPS, None, ALU.add).then_inc(s["var_ready"], 1)

            def normalise(i, to, y):
                dve.wait_ge(s["rstd_ready"], i + 1)
                return v.tensor_scalar(to, y, TMV[:, i % 2, 0:1], TRS[:, i % 2:i % 2 + 1], ALU.subtract, ALU.mult)

            def route(grp, part):
                row = lambda i: ROWS[:, i, :]
                wide = lambda i: ROWS[:, i, :, None].broadcast_to([P, GB, E])
                pr, eq, lg = PR[:, grp, :, :], EQ[:, grp, :, :], LG[:, grp, :, :]
                hots = HOT1[:, grp, :, :], HOT2[:, grp, :, :]
                dve.wait_ge(s["dve_link"], chain[0])
                if part == 0:
                    dve.wait_ge(s["router_full"], GB * (grp + 1))
                    router = ROUTER.rearrange("t (b e) -> t b e", b=GB)
                    link(v.tensor_reduce(row(0), router, axis=AX_X, op=ALU.max))
                    v.tensor_tensor(lg, router, wide(0), ALU.subtract).then_inc(s["router_read"], 1)
                elif part == 1:
                    dve.wait_ge(s["route_exp"], grp + 1)
                    link(v.tensor_reduce(row(1), pr, axis=AX_X, op=ALU.add))
                    link(v.reciprocal(row(2), row(1)))
                    mark(v.tensor_tensor(pr, pr, wide(2), ALU.mult))
                elif part in (2, 3):
                    k = part - 2
                    src = lg if k else pr
                    dve.wait_ge(s["consts"], 1)
                    link(v.tensor_reduce(row(3 + k), src, axis=AX_X, op=ALU.max))
                    link(v.tensor_tensor(eq, src, wide(3 + k), ALU.is_equal))
                    link(v.tensor_tensor(eq, eq, WTE[:, :, :], ALU.mult))
                    link(v.tensor_reduce(row(5), eq, axis=AX_X, op=ALU.max))
                    if k == 0:
                        link(v.tensor_tensor(hots[0], eq, wide(5), ALU.is_equal))
                        mark(v.scalar_tensor_tensor(lg, hots[0], -2.0, pr, ALU.mult, ALU.add))
                    else:
                        mark(v.tensor_tensor(hots[1], eq, wide(5), ALU.is_equal))
                else:
                    mark(v.tensor_tensor(row(6), row(3), row(4), ALU.add))
                    link(v.tensor_tensor(eq, hots[0], hots[1], ALU.add))
                    mark(v.reciprocal(row(7), row(6)))
                    link(v.tensor_tensor(eq, eq, pr, ALU.mult))
                    v.tensor_tensor(WT[:, grp, :, :], eq, wide(7), ALU.mult).then_inc(s["weights_ready"], 1)

            def scores_max(x):
                if x >= NU:
                    return
                b, u = unit(x)
                if u == 0 and b >= 2:
                    dve.wait_ge(s["mt_full"], b - 1)
                dve.wait_ge(s["sx_full"], x + 1)
                v.tensor_reduce(NMX2[:, b % 2, HU * u:HU * u + HU],
                                sx_bank(x)[:, :].rearrange("q (h k) -> q h k", h=HU),
                                axis=AX_X, op=ALU.max, negate=True).then_inc(s["maxx_done"], 1)

            def x_rest(x):
                if (b := due(x, UB, UB, B)) is not None:
                    dve.wait_ge(s["mxh_done"], b + 1)
                    if b:
                        dve.wait_ge(s["mt_done"], b)
                    v.tensor_tensor(MR[:, :], MX_T, MXT[:, b % 2, 0, :], ALU.subtract).then_inc(s["mxr_done"], 1)
                if (b := due(x, XTAIL + 1, UB, B)) is not None:
                    dve.wait_ge(s["px_read"], b + 1)
                    if b:
                        dve.wait_ge(s["sums_added"], b)
                    v.reciprocal(XR[:, :], PXS[:, b % 2, :, VC - 1]).then_inc(s["num_done"], 1)
                if (b := due(x, X2T + 1, UB, B)) is not None:
                    grp, half = divmod(b, GB)
                    dve.wait_ge(s["x2h_done"], b + 1)
                    c = slice(half * P, (half + 1) * P)
                    v.tensor_tensor(X2Tl[:, grp, c], TURNED, X2Th[:, grp, c].bitcast(F32),
                                    ALU.subtract).then_inc(s["x2l_done"], 1)
                if (b := due(x, XTAIL + 4, UB, B)) is not None:
                    normalise(B + b, X2[:, b, :], Y[:, b % 2, :]).then_inc(s["x2_normed"], 1)
                m = x - ST_LAG - 1
                if 0 <= m < NU and by_dve(m):
                    dve.wait_ge(s["e32_done"], m + 1)
                    if m >= 4:
                        dve.wait_ge(s["px_full"], m - 3)
                    v.tensor_tensor(EL[:, m % 4, :], E32[:, m % 2, :], EH[:, m % 4, :],
                                    ALU.subtract).then_inc(s["el_dve"], 1)
                if (b := due(x, XTAIL + 3, UB, B)) is not None:
                    dve.wait_ge(s["sums_added"], b + 1)
                    statistics(B + b, Y[:, b % 2, :])

            def x_route(x):
                for part in range(5):
                    first = UB * (GB - 1) + ROUTE
                    if (grp := due(x, first + (part + 1) // 2, UB * GB, 1)) is None:
                        grp = due(x, first + UB * GB + part, UB * GB, NG - 1)
                        grp = None if grp is None else grp + 1
                    if grp is not None:
                        route(grp, part)

            for n in range(STEPS):
                if n < NU:
                    dve.wait_ge(s["s_full"], n + 1)
                    v.tensor_reduce(NMX[:, n % 4, :], bank[S_BANK[n % 2]][:, :].rearrange("q (h k) -> q h k", h=HU),
                                    axis=AX_X, op=ALU.max, negate=True).then_inc(s["max_done"], 1)
                items = x_items(n)
                if items and n < NU:
                    scores_max(items[0])
                    x_rest(items[0])
                if n + TG < NT:
                    t_low(n + TG)
                if n < 2:
                    dve.wait_ge(s["oh_done"], n + 3)
                    low_weights(2 + n, O0 + 2 + n, Vh, Vl)
                k = n - PT_LAG
                if 0 <= k < NU:
                    dve.wait_ge(s["pt_full"], k + 1)
                    if k >= 3:
                        dve.wait_ge(s["pv_full"], k - 2)
                    v.tensor_copy(PTs[:, k % 3, :], bank[PT_BANK][:, :]).then_inc(s["pt_done"], 1)
                if (b := due(n, TAIL + 1, UB, B)) is not None:
                    normalise(b, X1[:, b, :], Y[:, b % 2, :])
                    if b:
                        dve.wait_ge(s["qt_full"], b)
                    normalise(b, QTN[:, :].rearrange("t (d h) -> t h d", h=H),
                              Y[:, b % 2, :].rearrange("t (h d) -> t h d", h=H)).then_inc(s["x_normed"], 1)
                if (b := due(n, TAIL, UB, B)) is not None:
                    dve.wait_ge(s["pv_full"], UB * b + UB)
                    v.tensor_tensor(Y[:, b % 2, :], bank[ACC][:, 0:D], X[:, b, :], ALU.add).then_inc(s["y_added"], 1)
                    dve.wait_ge(s["y_added"], b + 1)
                    statistics(b, Y[:, b % 2, :])
                if (b := due(n, q_step(0), UB, B)) is not None:
                    dve.wait_ge(s["qh_done"], b + 1)
                    v.scalar_tensor_tensor(QR[:, :], TURNED, float(XH) ** -0.5, QT[:, b % 2, 0, :], ALU.mult,
                                           ALU.subtract).then_inc(s["q_read"], 1)
                    dve.wait_ge(s["q_read"], b + 1)
                    link(v.tensor_copy(QT[:, b % 2, 1, :], QR[:, :]))
                    v.tensor_tensor(QT[:, b % 2, 2, :], QR[:, :], QT[:, b % 2, 1, :], ALU.subtract).then_inc(s["qt_done"], 1)
                if (b := due(n, k_step(0), 2, B)) is not None:
                    dve.wait_ge(s["kh_done"], b + 1)
                    if b:
                        dve.wait_ge(s["kt_done"], b)
                    v.tensor_tensor(KR[:, :], TURNED, KT[:, b % 2, 0, :], ALU.subtract).then_inc(s["kr_done"], 1)
                if n < NU:
                    dve.wait_ge(s["exp_done"], n + 1)
                    v.reciprocal(RCP[:, n % 4, :], SUM[:, n % 4, :]).then_inc(s["sum_recip"], 1)
                if items and n >= NU:
                    scores_max(items[0])
                    x_route(items[0])
                f = n - F0
                if 0 <= f < NF:
                    dve.wait_ge(s["tanh_done"], f + 1)
                    gated = SG[:, f % 2, :, :].rearrange("i c t -> i (c t)")
                    v.scalar_tensor_tensor(gated, gated, 1.0, bank[G_BANK][:, :], ALU.add,
                                           ALU.mult).then_inc(s["gated"], 1)
                if items and n >= NU:
                    x_rest(items[0])
                if items[1:]:
                    scores_max(items[1])
                if (w := due(n, W0, 1, 2 * UB)) is not None:
                    dve.wait_ge(s["wh_done"], w + 1)
                    es = slice(2 * (w % 4), 2 * (w % 4) + 2)
                    v.tensor_tensor(WL[w // 4][:, es, :], bank[T_BANK][:, :].rearrange("h (e i) -> h e i", e=2),
                                    WH[w // 4][:, es, :].bitcast(F32), ALU.subtract).then_inc(s["w_done"], 1)
                if 0 <= f < NF:
                    dve.wait_ge(s["gated"], f + 1)
                    dve.wait_ge(s["u_full"], f + 1)
                    if f >= 2:
                        dve.wait_ge(s["dn_full"], f - 1)
                    v.tensor_tensor(HT[:, f % 2, :, :].rearrange("i c t -> i (c t)"), bank[U_BANK][:, :], gated,
                                    ALU.mult).then_inc(s["hu_done"], 1)
                if items[1:]:
                    x_rest(items[1])
                    x_route(items[1])
                if (grp := due(n, F0 + E + 1, E, NG)) is not None:
                    dve.wait_ge(s["y_acc"], E * (grp + 1))
                    bs = range(GB * grp, GB * grp + GB)
                    for b in bs:
                        ins = v.bn_stats(BST[:, b, :], Z[:, b, :])
                    mark(ins)
                if (grp := due(n, F0 + E + 2, E, NG)) is not None:
                    bs = range(GB * grp, GB * grp + GB)
                    dve.wait_ge(s["dve_link"], chain[0])
                    for b in bs:
                        ins = v.bn_aggr(BMV[:, b, :], BST[:, b, :])
                    link(ins)
                    v.tensor_scalar(VE[:, bs[0]:bs[0] + GB], BMV[:, bs[0]:bs[0] + GB, 1], EPS, None,
                                    ALU.add).then_inc(s["last_var"], 1)
                if (grp := due(n, F0 + E + 3, E, NG)) is not None:
                    dve.wait_ge(s["last_rstd"], grp + 1)
                    for b in range(GB * grp, GB * grp + GB):
                        v.tensor_scalar(OUT[:, b, :], Z[:, b, :], BMV[:, b, 0:1], RS[:, b:b + 1], ALU.subtract,
                                        ALU.mult).then_inc(s["out_ready"], 1)

        @block.tensor
        def _(pe):
            mm = nc.tensor.matmul
            turn = nc.tensor.transpose

            def split_mm(out_ap, ah, al, bh, bl):
                mm(out_ap, ah, bh, start=True, stop=False)
                mm(out_ap, ah, bl, start=False, stop=False)
                return mm(out_ap, al, bh, start=False, stop=True)

            pe.wait_ge(s["ident"], 1)

            def room(i):
                if i >= 4:
                    j = i - 4
                    if X0 <= j < X0 + 2:
                        pe.wait_ge(s["xtf_done"], j - X0 + 1)
                    else:
                        pe.wait_ge(set_done[j], 1)

            def transposes(i, src):
                room(i)
                for j in range(4):
                    ins = turn(sbank(i)[:, j * P:(j + 1) * P], src(j), ID[:, :])
                ins.then_inc(s["setup_full"], 1)

            def weight_product(i0, i, wt, bd):
                room(i0 + i)
                for j in range(2):
                    c = 2 * i + j
                    ins = mm(sbank(i0 + i)[:, 2 * D * j:2 * D * (j + 1)], wt[:, c, :],
                             bd[:, c, :, :].rearrange("p j d -> p (j d)"), start=True, stop=True)
                ins.then_inc(s["setup_full"], 1)

            def t_product(t):
                grp, pair = divmod(t, TG)
                pe.wait_ge(s["xtl_done"], grp // 2 + 1)
                if t < TG:
                    b_ = bank[t % 2]
                    pe.wait_ge(set_done[M0 + pair // 2], 1)
                    if t >= 2:
                        pe.wait_ge(s["tl_done"], t - 1)
                else:
                    b_ = bank[T_BANK]
                    pe.wait_ge(s["tl_done"], t)
                c = slice(grp * GB * P, (grp + 1) * GB * P)
                for j in range(2):
                    h = 2 * pair + j
                    ins = split_mm(b_[:, GB * P * j:GB * P * (j + 1)], Mh[:, h, :], Ml[:, h, :], XTh[:, c], XTl[:, c])
                ins.then_inc(s["t_full"], 1)

            def x_item(n, x):
                if (b := due(x, UB, UB, B)) is not None:
                    pe.wait_ge(s["maxx_done"], UB * (b + 1))
                    if b:
                        pe.wait_ge(s["mxr_done"], b)
                    pe.wait_ge(s["q_read"], sum(q_step(i) < n + (n >= NU) for i in range(B)))
                    x2_before = sum(UB * i + X2T < x for i in range(B))
                    if x2_before:
                        pe.wait_ge(s["x2l_done"], x2_before)
                    routed = sum(UB * i + X2T + 3 < x for i in range(B)) // GB
                    if routed:
                        pe.wait_ge(s["router_read"], routed)
                    turn(MX_T, NMX2[:, b % 2, :], ID[:, :]).then_inc(s["mt_full"], 1)
                if 0 <= x < NU:
                    b, u = unit(x)
                    c = slice(b * P, (b + 1) * P)
                    if x == 0:
                        pe.wait_ge(s["kp_in"], 16 * (3 + B))
                        pe.wait_ge(s["one_rows"], 16)
                        pe.wait_ge(set_done[O0 + 3], 1)
                    elif SX_ALT < x <= SX_ONE:
                        pe.wait_ge(s["maxx_done"], x - 1)
                    else:
                        pe.wait_ge(s["maxx_done"], x)
                    if x == SX_ALT + 1:
                        pe.wait_ge(s["y_added"], B)
                    pe.wait_ge(q_in[b], 16)
                    for j in range(HU):
                        h = HU * u + j
                        ins = mm(sx_bank(x)[:, j * P:(j + 1) * P], QP[0:KMAX, h, c], KP[0:KMAX, h, c],
                                 start=True, stop=True)
                    ins.then_inc(s["sx_full"], 1)
                m = x - ST_LAG
                if 0 <= m < NU:
                    b, u = unit(m)
                    c = slice(b * P, (b + 1) * P)
                    if m < 2:
                        pe.wait_ge(s["exp_done"], NU - 1 + m)
                    else:
                        pe.wait_ge(s["e32_done"], m - 1)
                    pe.wait_ge(m_in[b], 16 * PARTS)
                    for j in range(HU):
                        h = HU * u + j
                        ins = mm(bank[ST_BANK[m % 2]][:, j * P:(j + 1) * P], KP[0:KALL, h, c], QP[0:KALL, h, c],
                                 start=True, stop=True)
                    ins.then_inc(s["st_full"], 1)
                m = x - PX_LAG
                if 0 <= m < NU:
                    b, u = unit(m)
                    pe.wait_ge(*el_done(m))
                    if u == 0:
                        pe.wait_ge(s["vparts_ready"], b + 1)
                        if b:
                            pe.wait_ge(s["px_read"], b)
                        else:
                            pe.wait_ge(s["consts"], 1)
                            pe.wait_ge(s["pt_done"], NU)
                    for j in range(HU):
                        h = HU * u + j
                        to = bank[PX_BANK][:, h * VC:(h + 1) * VC]
                        mm(to, EH[:, m % 4, j * P:(j + 1) * P], XV[:, b, h, :], start=True, stop=False)
                        ins = mm(to, EL[:, m % 4, j * P:(j + 1) * P], XV[:, b, h, :], start=False, stop=True)
                    ins.then_inc(s["px_full"], 1)
                if (b := due(x, X2T, UB, B)) is not None:
                    pe.wait_ge(s["x2_normed"], b + 1)
                    pe.wait_ge(s["mxr_done"], sum(UB * (i + 1) <= x for i in range(B)))
                    if b:
                        pe.wait_ge(s["x2l_done"], b)
                        if b // GB:
                            pe.wait_ge(s["router_read"], b // GB)
                    else:
                        pe.wait_ge(s["q_read"], B)
                    turn(TURNED, X2[:, b, :], ID[:, :]).then_inc(s["x2t_full"], 1)
                if (b := due(x, X2T + 3, UB, B)) is not None:
                    grp, half = divmod(b, GB)
                    pe.wait_ge(s["x2l_done"], b + 1)
                    pe.wait_ge(s["rw_split"], 2)
                    pe.wait_ge(s["mxr_done"], min(B, (x - 1) // UB))
                    if grp:
                        pe.wait_ge(s["router_read"], grp)
                    c = slice(half * P, (half + 1) * P)
                    split_mm(ROUTER[:, half * E:(half + 1) * E], X2Th[:, grp, c], X2Tl[:, grp, c],
                             RWh[:, :], RWl[:, :]).then_inc(s["router_full"], 1)

            def expert_in(f, gu):
                grp, e = divmod(f, E)
                if e == 0:
                    pe.wait_ge(s["x2l_done"], GB * (grp + 1))
                if f == 0:
                    pe.wait_ge(s["w_done"], 3 * UB)
                    pe.wait_ge(s["v_done"], NU)
                else:
                    pe.wait_ge(s["hu_done" if gu else "gated"], f)
                for i in range(2):
                    ic = slice(i * P, (i + 1) * P)
                    ins = split_mm(bank[(G_BANK, U_BANK)[gu]][:, i * GB * P:(i + 1) * GB * P], WH[gu][:, e, ic],
                                   WL[gu][:, e, ic], X2Th[:, grp, :], X2Tl[:, grp, :])
                ins.then_inc(s["u_full" if gu else "g_full"], 1)

            for i in range(2):
                pe.wait_ge(wk_in[i], 16)
                transposes(K0 + i, lambda j: WK[:, (4 * i + j) * P:(4 * i + j + 1) * P])
            pe.wait_ge(s["wq_in"], 16)
            for i in range(2):
                transposes(Q0 + i, lambda j: WQ[:, (4 * i + j) * P:(4 * i + j + 1) * P])
            for i in range(2):
                pe.wait_ge(s["xhat_done"], 4 * i + 4)
                transposes(X0 + i, lambda j: XHAT[:, 4 * i + j, :])
            for i in range(4):
                pe.wait_ge(set_done[K0 + i // 2], 1)
                pe.wait_ge(set_done[Q0 + i // 2], 1)
                weight_product(M0, i, WKT, WQBD)
            pe.wait_ge(s["wv_in"], 16)
            for i in range(2):
                transposes(WV0 + i, lambda j: WV[:, (4 * i + j) * P:(4 * i + j + 1) * P])
            for i in range(4):
                t_product(2 * i)
                t_product(2 * i + 1)
                if i == 0:
                    pe.wait_ge(s["wo_in"], 32)
                    pe.wait_ge(set_done[WV0], 1)
                    pe.wait_ge(set_done[WV0 + 1], 1)
                if i < 2:
                    weight_product(O0, i, WVT, WOBD)

            for n in range(STEPS):
                if n < NU:
                    b, u = unit(n)
                    c = slice(b * P, (b + 1) * P)
                    grp = b // GB
                    if n < 2:
                        pe.wait_ge(set_done[O0 + n], 1)
                    else:
                        pe.wait_ge(s["exp_done"], n - 1)
                    pe.wait_ge(s["tl_done"], TG * grp + 2 * u + 2)
                    t_of = lambda T: T[:, grp % 2, b % GB, HU * u:HU * u + HU, :].rearrange("d h k -> d (h k)")
                    split_mm(bank[S_BANK[n % 2]][:, :], XTh[:, c], XTl[:, c], t_of(Th), t_of(Tl)).then_inc(s["s_full"], 1)
                items = x_items(n)
                if items and n < NU:
                    x_item(n, items[0])
                if n + TG < NT:
                    t_product(n + TG)
                if n < 2:
                    weight_product(O0, 2 + n, WVT, WOBD)
                k = n - PT_LAG
                if 0 <= k < NU:
                    b, u = unit(k)
                    c = slice(b * P, (b + 1) * P)
                    if k == 0:
                        pe.wait_ge(s["tl_done"], TG)
                    else:
                        pe.wait_ge(s["v_done"], k)
                    pe.wait_ge(set_done[O0 + u], 1)
                    v_of = lambda V: V[:, HU * u:HU * u + HU, :].rearrange("d h n -> d (h n)")
                    split_mm(bank[V_BANK][:, :], XTh[:, c], XTl[:, c], v_of(Vh), v_of(Vl)).then_inc(s["v_full"], 1)
                    pe.wait_ge(s["p_norm"], k + 1)
                    if k:
                        pe.wait_ge(s["pt_done"], k)
                    else:
                        pe.wait_ge(set_done[O0 + 2], 1)
                    for j in range(HU):
                        ins = turn(bank[PT_BANK][:, j * P:(j + 1) * P], EX[:, k % 3, j * P:(j + 1) * P], ID[:, :])
                    ins.then_inc(s["pt_full"], 1)
                k = n - PV_LAG
                if 0 <= k < NU:
                    b, u = unit(k)
                    pe.wait_ge(s["pt_done"], k + 1)
                    pe.wait_ge(s["v_done"], k + 1)
                    if u == 0 and b:
                        pe.wait_ge(s["y_added"], b)
                    for j in range(HU):
                        ins = mm(bank[ACC][:, 0:D], PTs[:, k % 3, j * P:(j + 1) * P], VP[:, k % 3, j * D:(j + 1) * D],
                                 start=u == 0 and j == 0, stop=u == UB - 1 and j == HU - 1)
                    ins.then_inc(s["pv_full"], 1)
                if (b := due(n, k_step(0), 2, B)) is not None:
                    if b:
                        pe.wait_ge(s["kr_done"], b)
                    else:
                        pe.wait_ge(s["ck_turned"], 1)
                    q_before = sum(q_step(i) < n for i in range(B))
                    if q_before:
                        pe.wait_ge(s["q_read"], q_before)
                    turn(TURNED, CKT[:, b, :], ID[:, :]).then_inc(s["kt_full"], 1)
                if (b := due(n, q_step(0), UB, B)) is not None:
                    pe.wait_ge(s["x_normed"], b + 1)
                    pe.wait_ge(s["kr_done"], sum(k_step(i) <= n for i in range(B)))
                    if b:
                        pe.wait_ge(s["q_read"], b)
                    mx_before = sum(UB * (i + 1) < (x_items(n) or (0,))[0] + (n < NU) for i in range(B))
                    if mx_before:
                        pe.wait_ge(s["mxr_done"], mx_before)
                    turn(TURNED, QTN[:, :], ID[:, :]).then_inc(s["qt_full"], 1)
                f = n - F0
                if 0 <= f < NF:
                    expert_in(f, 0)
                if items and n >= NU:
                    x_item(n, items[0])
                if (w := due(n, W0, 1, 3 * UB)) is not None:
                    if w == 0:
                        pe.wait_ge(s["tl_done"], NT)
                    else:
                        pe.wait_ge(s["w_done"], w)
                    pe.wait_ge(s[("gate_in", "up_in", "down_in")[w // 4]], 16)
                    for j in range(4):
                        if w < 8:
                            src = (GRAW if w < 4 else URAW)[:, 4 * (w % 4) + j, :]
                        else:
                            src = DRAW[:, 2 * (w - 8) + j // 2, j % 2, :]
                        ins = turn(bank[T_BANK][:, j * P:(j + 1) * P], src, ID[:, :])
                    ins.then_inc(s["w_full"], 1)
                if 0 <= f < NF:
                    expert_in(f, 1)
                if items[1:]:
                    x_item(n, items[1])
                f = n - F0 - 1
                if 0 <= f < NF:
                    grp, e = divmod(f, E)
                    pe.wait_ge(s["hu_done"], f + 1)
                    if f > Y_ALT:
                        pe.wait_ge(s["y_read"], f - 1)
                        pe.wait_ge(s["maxx_done"], NU)
                    elif f:
                        pe.wait_ge(s["y_read"], f)
                    else:
                        pe.wait_ge(s["maxx_done"], SX_ONE)
                        pe.wait_ge(s["w_done"], 3 * UB)
                    for h2 in range(GB):
                        for i in range(2):
                            ins = mm(y_bank(f)[:, h2 * D:(h2 + 1) * D], HT[:, f % 2, i, h2 * P:(h2 + 1) * P],
                                     WD[:, e, i, :], start=i == 0, stop=i == 1)
                    ins.then_inc(s["dn_full"], 1)


_INS = ["x", "ctx_2048", "itok_Bx1_68_817", "L0_attn_ln_gamma", "L0_attn_ln_beta", "L0_attn_Wq", "L0_attn_Wk",
        "L0_attn_Wv", "L0_attn_Wo", "L0_xattn_b", "L0_ffn_router_w", "L0_ffn_gate_w", "L0_ffn_up_w", "L0_ffn_down_w"]


def kernel(**inputs):
    import numpy as np
    import concourse.bacc as bacc
    from concourse.bass_utils import run_bass_kernel_spmd

    nc = bacc.Bacc("TRN2", target_bir_lowering=False, num_devices=1)
    arrays, args = {}, []
    for name in _INS:
        a = np.ascontiguousarray(inputs[name])
        arrays[f"in_{name}"] = a
        args.append(nc.dram_tensor(f"in_{name}", a.shape, mybir.dt.from_np(a.dtype), kind="ExternalInput").ap())
    args.append(nc.dram_tensor("out_0", (B, P, D), F32, kind="ExternalOutput").ap())
    decoder_layer(nc, *args)
    r = run_bass_kernel_spmd(nc, [arrays], core_ids=[0])
    return r.results[0]["out_0"]
```
